# Optimizing a Trainium2 kernel written in Bass

```python
import numpy as np
import jax
import jax.numpy as jnp

def _softmax(x, axis=-1):
    return jax.nn.softmax(x, axis=axis)

def _gelu(x):
    return jax.nn.gelu(x, approximate=True)

def _silu(x):
    return jax.nn.silu(x)

def _sigmoid(x):
    return jax.nn.sigmoid(x)

def _layernorm(x, axis=-1, eps=1e-05):
    m = jnp.mean(x, axis=axis, keepdims=True)
    v = jnp.var(x, axis=axis, keepdims=True)
    return (x - m) / jnp.sqrt(v + eps)

def _scatter_add(tgt, idx, src, axis=0):
    return tgt.at[idx].add(src)

def _segment_sum(src, seg, n):
    return jax.ops.segment_sum(src, seg, n)
kernel_name = 'mk_xattn_ffn_d1_seqx_r8_fc8fdf'

def setup_inputs(seed: int=0):
    np.random.seed(seed)
    _w = jnp.asarray

    def _rec_inputs():
        import jax
        import jax.numpy as jnp
        _rk = jax.random.key(seed)
        x = 7.22e-05 + 1 * jax.random.normal(jax.random.fold_in(_rk, 1), (16, 64, 256), jnp.float32)
        _lenS = 64 - jax.random.randint(jax.random.fold_in(_rk, 7), (16,), 0, max(1, 64 // 4) + 1, jnp.int32)
        _lenS2 = 64 - jax.random.randint(jax.random.fold_in(_rk, 8), (16,), 0, max(1, 64 // 4) + 1, jnp.int32)
        _ctx_2048P = jax.random.normal(jax.random.fold_in(_rk, 11), (16, 16, 256), jnp.float32)
        _ctx_2048c = jax.random.dirichlet(jax.random.fold_in(_rk, 511), 0.3 * jnp.ones((16,), jnp.float32), (16, 64))
        _ctx_2048t = jnp.einsum('bsk,bkd->bsd', _ctx_2048c, _ctx_2048P)
        _ctx_2048t = _ctx_2048t * jax.lax.rsqrt(jnp.mean(jnp.square(_ctx_2048t)) + 1e-12) * 0.953939
        ctx_2048 = 4.13588e-05 + 0.999923 * (_ctx_2048t + 0.3 * jax.random.normal(jax.random.fold_in(_rk, 611), (16, 64, 256), jnp.float32))
        return (x, ctx_2048)
    x, ctx_2048 = _rec_inputs()

    def _L0_xattn_setup():
        import jax, jax.numpy as jnp
        import numpy as np
        N, E, T, H = (8, 64, 256, 8)
        key = jax.random.key(seed)
        ks = jax.random.split(key, 6)
        s = 1.0 / np.sqrt(E)
        return {'mask': jax.random.normal(ks[0], (N, E, T), jnp.float32), 'encodings': jax.random.normal(ks[1], (N, E, T), jnp.float32), 'w_in': jax.random.normal(ks[2], (3 * E, E), jnp.float32) * s, 'b_in': jnp.zeros((3 * E,), jnp.float32), 'w_out': jax.random.normal(ks[3], (E, E), jnp.float32) * s, 'b_out': jnp.zeros((E,), jnp.float32), 'w_ct': jax.random.normal(ks[4], (E, E), jnp.float32) * s, 'b_ct': jnp.zeros((E,), jnp.float32), 'local_size': 64}
    _L0_xattn_all = _L0_xattn_setup()
    _L0_xattn_in = {k: v for k, v in _L0_xattn_all.items() if k in ('w_in', 'b_in', 'w_out', 'b_out', 'w_ct', 'b_ct')}
    del _L0_xattn_all

    def _L0_ffn_setup():
        import jax, jax.numpy as jnp
        import numpy as np
        B, S, DIM = (2, 256, 256)
        INTER = 128
        E = 8
        K = 2
        N_SHARED = 1
        ROUTE_SCALE = 1.0
        key = jax.random.key(seed)
        ks = jax.random.split(key, 8)
        s_in = 1.0 / np.sqrt(DIM)
        s_hid = 1.0 / np.sqrt(INTER)
        return {'x': jax.random.normal(ks[0], (B, S, DIM), dtype=jnp.float32), 'gate_w': jax.random.normal(ks[1], (E, DIM), dtype=jnp.float32) * s_in, 'w1': jax.random.normal(ks[2], (E, INTER, DIM), dtype=jnp.float32) * s_in, 'w2': jax.random.normal(ks[3], (E, DIM, INTER), dtype=jnp.float32) * s_hid, 'w3': jax.random.normal(ks[4], (E, INTER, DIM), dtype=jnp.float32) * s_in, 'ws1': jax.random.normal(ks[5], (N_SHARED * INTER, DIM), dtype=jnp.float32) * s_in, 'ws2': jax.random.normal(ks[6], (DIM, N_SHARED * INTER), dtype=jnp.float32) * s_hid, 'ws3': jax.random.normal(ks[7], (N_SHARED * INTER, DIM), dtype=jnp.float32) * s_in}
    _L0_ffn_all = _L0_ffn_setup()
    _L0_ffn_in = {k: v for k, v in _L0_ffn_all.items() if k in ('gate_w', 'w1', 'w2', 'w3', 'ws1', 'ws2', 'ws3')}
    del _L0_ffn_all
    return {'x': x, 'ctx_2048': ctx_2048, 'L0_xattn_w_in': _L0_xattn_in['w_in'], 'L0_xattn_b_in': _L0_xattn_in['b_in'], 'L0_xattn_w_out': _L0_xattn_in['w_out'], 'L0_xattn_b_out': _L0_xattn_in['b_out'], 'L0_xattn_w_ct': _L0_xattn_in['w_ct'], 'L0_xattn_b_ct': _L0_xattn_in['b_ct'], 'L0_ffn_gate_w': _L0_ffn_in['gate_w'], 'L0_ffn_w1': _L0_ffn_in['w1'], 'L0_ffn_w2': _L0_ffn_in['w2'], 'L0_ffn_w3': _L0_ffn_in['w3'], 'L0_ffn_ws1': _L0_ffn_in['ws1'], 'L0_ffn_ws2': _L0_ffn_in['ws2'], 'L0_ffn_ws3': _L0_ffn_in['ws3']}

def reference(x, ctx_2048, L0_xattn_w_in, L0_xattn_b_in, L0_xattn_w_out, L0_xattn_b_out, L0_xattn_w_ct, L0_xattn_b_ct, L0_ffn_gate_w, L0_ffn_w1, L0_ffn_w2, L0_ffn_w3, L0_ffn_ws1, L0_ffn_ws2, L0_ffn_ws3):
    import jax
    import jax.numpy as jnp

    def _L0_xattn_ref(mask, encodings, w_in, b_in, w_out, b_out, w_ct, b_ct, local_size):
        import jax, jax.numpy as jnp
        import numpy as np
        N, E, T, H = (8, 64, 256, 8)
        n, e, t = mask.shape
        d = e // H
        x = jnp.transpose(mask, (0, 2, 1))
        qkv = x @ w_in.T + b_in
        q, k, v = jnp.split(qkv, 3, axis=-1)
        q = q.reshape(n, t, H, d)
        k = k.reshape(n, t, H, d)
        v = v.reshape(n, t, H, d)
        scores = jnp.einsum('bqhd,bkhd->bhqk', q, k) / jnp.sqrt(jnp.asarray(d, q.dtype))
        idx = jnp.arange(t)
        band = jnp.abs(idx[:, None] - idx[None, :]) <= local_size
        neg = jnp.asarray(jnp.finfo(scores.dtype).min, scores.dtype)
        scores = jnp.where(band[None, None], scores, neg)
        attn = jax.nn.softmax(scores, axis=-1)
        o = jnp.einsum('bhqk,bkhd->bqhd', attn, v).reshape(n, t, e)
        o = o @ w_out.T + b_out
        o = jnp.transpose(o, (0, 2, 1))
        y = jax.nn.relu(o) * encodings
        out = jnp.einsum('nit,io->not', y, w_ct) + b_ct[None, :, None]
        return out

    def _L0_ffn_ref(x, gate_w, w1, w2, w3, ws1, ws2, ws3):
        import jax, jax.numpy as jnp
        import numpy as np
        B, S, DIM = (2, 256, 256)
        INTER = 128
        E = 8
        K = 2
        N_SHARED = 1
        ROUTE_SCALE = 1.0
        shape = x.shape
        xf = x.reshape(-1, DIM)
        scores = jax.nn.softmax(xf @ gate_w.T, axis=-1)
        weights, idx = jax.lax.top_k(scores, K)
        weights = weights * ROUTE_SCALE
        h = jnp.einsum('td,eid->eti', xf, w1)
        g = jax.nn.silu(h) * jnp.einsum('td,eid->eti', xf, w3)
        eo = jnp.einsum('eti,edi->etd', g, w2)
        comb = jnp.einsum('tke,tk->te', jax.nn.one_hot(idx, E, dtype=xf.dtype), weights)
        y = jnp.einsum('etd,te->td', eo, comb)
        z = jax.nn.silu(xf @ ws1.T) * (xf @ ws3.T) @ ws2.T
        return (y + z).reshape(shape)
    x = x + _L0_xattn_ref(_layernorm(x, axis=-1), ctx_2048, L0_xattn_w_in, L0_xattn_b_in, L0_xattn_w_out, L0_xattn_b_out, L0_xattn_w_ct, L0_xattn_b_ct, 64)
    x = x + _L0_ffn_ref(_layernorm(x, axis=-1), L0_ffn_gate_w, L0_ffn_w1, L0_ffn_w2, L0_ffn_w3, L0_ffn_ws1, L0_ffn_ws2, L0_ffn_ws3)
    return x

_drawn_inputs = setup_inputs


def setup_inputs(seed=0):
    import zlib

    import numpy as np

    out = dict(_drawn_inputs(seed))
    spreads = {'L0_xattn_b_in': (0.0, 0.1), 'L0_xattn_b_out': (0.0, 0.1), 'L0_xattn_b_ct': (0.0, 0.1)}
    factors = {}
    for name, (base, spread) in spreads.items():
        noise = np.random.default_rng([zlib.crc32(name.encode()), seed]).standard_normal(out[name].shape)
        drawn = base * np.exp(spread * noise) if base else spread * noise
        out[name] = jnp.asarray(drawn.astype(out[name].dtype))
    for name, factor in factors.items():
        out[name] = (out[name] * factor).astype(out[name].dtype)
    return out
```

```python
from contextlib import ExitStack

import concourse.bass as bass
from concourse import mybir

F32 = mybir.dt.float32
BF16 = mybir.dt.bfloat16
U32 = mybir.dt.uint32
ALU = mybir.AluOpType
ACT = mybir.ActivationFunctionType

P = 128
B, C, T = 16, 64, 256
PAIRS = B * C // P
HALVES = 4 * PAIRS
H, D = 8, 8
HG = 4
BAND = 64
W = P + BAND
NE, INTER = 8, 128
PARTS = 3
SPAN = PARTS * D
MROW = 96
EPS = 1e-5
NEG = -3.0e38
SLOTS = 5
LOADS = 2 * PARTS + 1
LOOP_LO, LOOP_HI = 2, PAIRS - 2


def experts_of(s):
    return [NE] if s == 0 else [2 * s - 2, 2 * s - 1]


class Link:

    def __init__(self, eng, sem):
        self.eng, self.sem, self.base, self.n = eng, sem, 0, 0

    def __call__(self, ins):
        self.n += 1
        ins.then_inc(self.sem, 1)
        return self.n

    def wait(self, wait_ge=None):
        (wait_ge or type(self.eng).wait_ge)(self.eng, self.sem, self.base + self.n)

    def enter(self, i, per):
        self.start, self.per = self.base + self.n, per
        self.base, self.n = (i - LOOP_LO) * per + self.start, 0

    def leave(self):
        assert self.n == self.per, f"{self.n} links in an iteration"
        self.base, self.n = self.start + (LOOP_HI - LOOP_LO) * self.per, 0


HELD = {mybir.EngineType.SP: "sync", mybir.EngineType.Pool: "pool", mybir.EngineType.DVE: "vector", mybir.EngineType.PE: "tensor",
        mybir.EngineType.Activation: "scalar"}


def build(nc, x, ctx_in, w_qkT, b_qk, w_vT, b_v, w_oT, b_o, w_ct, b_ct, gate_wT, w1T, w3T, w2T, ws1T, ws3T, ws2T, out):
    with ExitStack() as st:
        def sb(name, shape, dt=F32):
            return st.enter_context(nc.sbuf_tensor(name, shape, dt))

        def ps(name, shape):
            return st.enter_context(nc.psum_tensor(name, shape, F32))

        def sem(name):
            return st.enter_context(nc.semaphore(name))

        s_ps = ps("s_ps", [P, 2, 512])
        st_ps = ps("st_ps", [P, 2, 512])
        h_ps = ps("h_ps", [P, 512])
        y_ps = ps("y_ps", [P, 512])
        pv_ps = ps("pv_ps", [P, 512])
        m_ps = ps("m_ps", [P, 512])

        q_dram = nc.dram_tensor("q_parts", (2, PARTS, D * H, T), BF16, kind="Internal").ap()
        k_dram = nc.dram_tensor("k_parts", (2, 2 * PARTS - 1, D * H, T), BF16, kind="Internal").ap()

        wqk = sb("wqk", [P, 2, P])
        bqk = sb("bqk", [P, 2])
        wv = sb("wv", [P, P])
        bv = sb("bv", [P, 2, P])
        wo = sb("wo", [P, 2, C])
        wct = sb("wct", [P, P])
        bct = sb("bct", [P, 1])
        gw = sb("gw", [P, 2, NE])
        w1 = sb("w1", [P, 2, (NE + 1) * INTER])
        w3 = sb("w3", [P, 2, (NE + 1) * INTER])
        w2 = sb("w2", [P, NE + 1, T])
        ident = sb("ident", [P, P])
        identb = sb("identb", [P, P], BF16)
        band = sb("band", [P, 2, W])
        iota8 = sb("iota8", [P, NE])
        mhalf = sb("mhalf", [P, 1])
        zrows = sb("zrows", [PARTS, HG * T], BF16)

        xin = sb("xin", [P, T])
        xn = sb("xn", [P, T])
        stat1, mv1, ve1, rs1 = sb("stat1", [P, 6]), sb("mv1", [P, 2]), sb("ve1", [P, 1]), sb("rs1", [P, 1])
        parts = sb("parts", [P, PARTS, 2, T], BF16)
        rest = sb("rest", [P, 2, T])
        qs = sb("qs", [P, 4, HG, T], BF16)
        ks = sb("ks", [P, 4, HG, T], BF16)
        masked = sb("masked", [P, 8, W])
        mx = sb("mx", [P, 2, 2 * HG])
        mparts = sb("mparts", [P, 2, PARTS, 2 * HG], BF16)
        mrest = sb("mrest", [P, 2 * HG])
        mt = sb("mt", [PARTS * 2 * HG, 2, P], BF16)
        pt = sb("pt", [P, 2, 2, HG, W])
        v = sb("v", [P, 2, 2, H, 32])
        o1 = sb("o1", [P, 16, 32])
        rden = sb("rden", [P, 16])
        o2 = sb("o2", [P, 16, 32])
        oT = sb("oT", [P, 2, 2 * T])

        ctx = sb("ctx", [P, T])
        xres = sb("xres", [P, T])
        y = sb("y", [P, T])
        x2 = sb("x2", [P, T])
        stat2, mv2, ve2, rs2 = sb("stat2", [P, 6]), sb("mv2", [P, 2]), sb("ve2", [P, 1]), sb("rs2", [P, 1])
        xn2 = sb("xn2", [P, T])
        xn2T = sb("xn2T", [P, 2, P])
        gT = sb("gT", [NE, P])
        gtop, gdif, gexp, gsum, grec = (sb("gtop", [P, 8]), sb("gdif", [P, NE]), sb("gexp", [P, NE]),
                                        sb("gsum", [P, 1]), sb("grec", [P, 1]))
        prob, ptop, pidx, pidf = sb("prob", [P, NE]), sb("ptop", [P, 8]), sb("pidx", [P, 8], U32), sb("pidf", [P, 2])
        pick, comb, combT, crow, cb = (sb("pick", [P, 2, NE]), sb("comb", [P, NE]), sb("combT", [NE, P]),
                                       sb("crow", [1, NE * P]), sb("cb", [P, NE * P]))
        th, u, g = sb("th", [P, 2 * P]), sb("u", [P, 2 * P]), sb("g", [P, 2, 2 * P])
        gwt = sb("gwt", [P, 2, 2, P])
        res = sb("res", [P, T])

        NAMES = """x_in ctx_in w_qk_in w_v_in w_o_in w_ct_in w_gate_in w_ffn_in parts_out row_in crow_in out_done
            consts_ready zeros_ready ident_ready ks_ready
            ve1_ready rs1_ready xn_ready v_done v_ready qk_done part1_ready rest_ready part2_ready parts_ready
            s_done max_done mparts_ready mt_done mt_ready st_done exp_done band_done pv_done pv_read
            oT_ready o_done y_ready ct_done x2_ready ve2_ready rs2_ready xn2_ready xt_done xt_ready
            gt_done gt_ready g_done gdif_ready gexp_ready comb_ready combt_done combt_ready cb_ready
            up_done tanh_done hidden_ready gated_ready down_done res_ready dve_link pool_link held_sync held_pool held_vector held_tensor held_scalar""".split()
        S = {n: sem(n) for n in NAMES}
        loaded = [sem(f"loaded{j}") for j in range(4)]

        def wait(eng, s, r, value, alone=False):
            i, low = r
            if value(low) > 0:
                (hold if alone or eng.engine == mybir.EngineType.SP else type(eng).wait_ge)(eng, S[s] if isinstance(s, str) else s, value(i))

        def hold(eng, sem, value):
            eng.wait_ge(sem, value).then_inc(S["held_" + HELD[eng.engine]], 1)

        def wait(eng, s, r, value, alone=False):
            i, low = r
            if value(low) > 0:
                (hold if alone or eng.engine == mybir.EngineType.SP else type(eng).wait_ge)(eng, S[s] if isinstance(s, str) else s, value(i))

        def run(eng, body, link=None, per=0):
            for i in range(-1, LOOP_LO):
                body((i, i))
            with eng.Fori(LOOP_LO, LOOP_HI) as i:
                if link:
                    link.enter(i, per)
                body((i, LOOP_LO))
                if link:
                    link.leave()
            for i in range(LOOP_HI, PAIRS + 2):
                body((i, i))

        def has_half(k):
            return 0 <= k < HALVES

        def has_pair(p):
            return 0 <= p < PAIRS

        def slots_in(low, j):
            todo = {0: [(-2, 3)], 1: [(-2, 4)], 2: [(-1, 0), (-1, 1)], 3: [(-1, 2)]}[j]
            return [(o, s) for o, s in todo if has_pair(low + o)]

        block = st.enter_context(nc.Block())

        @block.sync
        def _(sp):
            sp.dma_start(xin[:, :], x[0:P, :]).then_inc(S["x_in"], 16)
            sp.wait_ge(S["zeros_ready"], 2)
            for b in range(2):
                c = slice(C * b, C * b + C)
                for t in range(2):
                    sp.dma_start(wqk[c, t, c], w_qkT[:, C * t:C * t + C]).then_inc(S["w_qk_in"], 16)
                    sp.dma_start(bqk[c, t:t + 1], b_qk[C * t:C * t + C, :]).then_inc(S["w_qk_in"], 16)
            for b in range(2):
                c = slice(C * b, C * b + C)
                sp.dma_start(wv[c, c], w_vT).then_inc(S["w_v_in"], 16)
                for kt in range(2):
                    sp.dma_start(bv[:, kt, c], b_v.to_broadcast([P, C])).then_inc(S["w_v_in"], 16)

            def stacks(i, low, k):
                off = k
                slot = off % 4
                b, hh = slot // 2, slot % 2
                pair = (i + off // 4, low + off // 4)
                wait(sp, "st_done", (i, low), lambda i: 4 * (4 * i + off - 4 + 1))
                wait(sp, "parts_out", pair, lambda p: 16 * 6 * (p + 1))
                if pair[1] == 0:
                    sp.wait_ge(S["zeros_ready"], 6)
                    sp.wait_ge(S["ks_ready"], 1)
                for r in range(PARTS):
                    rows = slice(SPAN * r, SPAN * r + SPAN)
                    qv = q_dram[b].rearrange("a (d h) t -> (a d) h t", h=H)[:, HG * hh:HG * hh + HG, :]
                    kv = k_dram[b].rearrange("a (d h) t -> (a d) h t", h=H)[D * r:D * r + SPAN, HG * hh:HG * hh + HG, :]
                    sp.dma_start(qs[rows, slot, :, :], qv).then_inc(loaded[slot], 16)
                    sp.dma_start(ks[rows, slot, :, :], kv).then_inc(loaded[slot], 16)
                sp.dma_start(qs[MROW:MROW + PARTS, slot, :, :], zrows[:, :].rearrange("a (h t) -> a h t", h=HG)).then_inc(loaded[slot], 16)

            def body(r):
                i, low = r
                for j in range(4):
                    k, klow = 4 * i + j, 4 * low + j
                    if has_half(klow + 1):
                        off = j + 1
                        slot, par = off % 4, off % 2
                        wait(sp, "mt_ready", r, lambda i: 4 * i + off + 1)
                        for a in range(PARTS):
                            dst = qs[MROW + a:MROW + a + 1, slot, :, :].rearrange("a h (q t) -> a (h q) t", q=2)
                            sp.dma_start(dst, mt[2 * HG * a:2 * HG * a + 2 * HG, par, :]).then_inc(S["row_in"], 16)
                    if j == 1 and has_pair(low + 1):
                        wait(sp, "parts_ready", r, lambda i: i + 2, alone=True)
                        wait(sp, loaded[3], r, lambda i: 16 * LOADS * (i + 1), alone=True)
                        for b in range(2):
                            rows = slice(C * b, C * b + C)
                            q_to, k_to = (t[b].rearrange("a r t -> r a t") for t in (q_dram, k_dram))
                            sp.dma_start(q_to, parts[rows, :, 0, :]).then_inc(S["parts_out"], 16)
                            sp.dma_start(k_to[:, 0:PARTS, :], parts[rows, :, 1, :]).then_inc(S["parts_out"], 16)
                            sp.dma_start(k_to[:, PARTS:, :], parts[rows, 0:PARTS - 1, 1, :]).then_inc(S["parts_out"], 16)
                    if has_half(klow + 3):
                        stacks(i, low, j + 3)
                    if j == 1 and has_pair(low + 2):
                        wait(sp, "xn_ready", r, lambda i: i + 2, alone=True)
                        sp.dma_start(xin[:, :], x[bass.ds((i + 2) * P, P), :]).then_inc(S["x_in"], 16)
                    if j == 2 and has_pair(low):
                        wait(sp, "x2_ready", r, lambda i: i, alone=True)
                        sp.dma_start(ctx[:, :], ctx_in[bass.ds(i * P, P), :]).then_inc(S["ctx_in"], 16)
                        sp.dma_start(xres[:, :], x[bass.ds(i * P, P), :]).then_inc(S["ctx_in"], 16)
                    if j == 2 and has_pair(low - 1):
                        wait(sp, "combt_ready", r, lambda i: i)
                        wait(sp, "cb_ready", r, lambda i: i - 1)
                        sp.dma_start(crow[:, :].rearrange("a (e t) -> a e t", e=NE), combT[:, :]).then_inc(S["crow_in"], 16)
                    if j == 1 and has_pair(low - 2):
                        wait(sp, "res_ready", r, lambda i: i - 1, alone=True)
                        sp.dma_start(out[bass.ds((i - 2) * P, P), :], res[:, :]).then_inc(S["out_done"], 16)

            run(sp, body)
            sp.wait_ge(S["out_done"], 16 * PAIRS)

        @block.scalar
        def _(act):
            act.wait_ge(S["zeros_ready"], 4)
            for h in range(H):
                act.dma_start(wo[32 * (h % HG):32 * (h % HG) + D, h // HG, :], w_oT[D * h:D * h + D, :]).then_inc(S["w_o_in"], 16)
            act.dma_start(wo[D:D + 1, 0, :], b_o).then_inc(S["w_o_in"], 16)
            for b in range(2):
                c = slice(C * b, C * b + C)
                act.dma_start(wct[c, c], w_ct).then_inc(S["w_ct_in"], 16)
                act.dma_start(bct[c, :], b_ct).then_inc(S["w_ct_in"], 16)
            act.dma_start(gw[:, :, :], gate_wT.rearrange("(c p) e -> p c e", p=P)).then_inc(S["w_gate_in"], 16)
            for w_sb, big, shared in ((w1, w1T, ws1T), (w3, w3T, ws3T)):
                act.dma_start(w_sb[:, :, 0:NE * INTER], big.rearrange("(c p) e -> p c e", p=P)).then_inc(S["w_ffn_in"], 16)
                act.dma_start(w_sb[:, :, NE * INTER:], shared.rearrange("(c p) e -> p c e", p=P)).then_inc(S["w_ffn_in"], 16)
            act.dma_start(w2[:, 0:NE, :], w2T).then_inc(S["w_ffn_in"], 16)
            act.dma_start(w2[:, NE, :], ws2T).then_inc(S["w_ffn_in"], 16)

            def exp(r, j, n):
                i, low = r
                kt, g0 = n // 2, 2 * (n % 2)
                wait(act, "st_done", r, lambda i: 4 * (4 * i + j) + n + 1)
                if n == 0:
                    wait(act, "pv_done", r, lambda i: 4 * i + j - 1)
                act.activation(pt[:, j % 2, kt, g0:g0 + 2, :], st_ps[:, n % 2, 0:2 * W].rearrange("p (h w) -> p h w", h=2),
                               ACT.Exp, scale=float(D) ** -0.5).then_inc(S["exp_done"], 1)

            def max_rows(r, j):
                wait(act, "mt_done", r, lambda i: 4 * i + j + 2)
                wait(act, "row_in", r, lambda i: 16 * PARTS * (4 * i + j))
                act.copy(mt[:, (j + 1) % 2, :], m_ps[0:PARTS * 2 * HG, 0:P]).then_inc(S["mt_ready"], 1)

            def tanh(r, o, s):
                n = len(experts_of(s)) * P
                wait(act, "up_done", r, lambda i: SLOTS * (i + o) + s + 1)
                wait(act, "hidden_ready", r, lambda i: SLOTS * (i + o) + s)
                act.activation(th[:, 0:n], h_ps[:, 0:n], ACT.Tanh, scale=0.5).then_inc(S["tanh_done"], 1)

            def body(r):
                i, low = r
                for j in range(4):
                    here, rows = has_half(4 * low + j), has_half(4 * low + j + 1)
                    slots = slots_in(low, j)
                    if here:
                        exp(r, j, 0)
                    if rows:
                        max_rows(r, j)
                    if j == 2 and has_pair(low - 1):
                        wait(act, "xt_done", r, lambda i: i)
                        wait(act, "up_done", r, lambda i: SLOTS * (i - 1))
                        act.copy(xn2T[:, :, :].rearrange("p c t -> p (c t)"), m_ps[:, 0:2 * P]).then_inc(S["xt_ready"], 1)
                    if j in (0, 1):
                        for o, s in slots:
                            tanh(r, o, s)
                    if here:
                        exp(r, j, 1)
                    if j == 2 and has_pair(low - 1):
                        wait(act, "gt_done", r, lambda i: i)
                        act.copy(gT[:, :], m_ps[0:NE, 0:P]).then_inc(S["gt_ready"], 1)
                        tanh(r, -1, 0)
                    if j == 3:
                        for o, s in slots:
                            tanh(r, o, s)
                    if here:
                        exp(r, j, 2)
                    if j == 2 and has_pair(low - 1):
                        wait(act, "gdif_ready", r, lambda i: i)
                        act.activation(gexp[:, :], gdif[:, :], ACT.Exp, accum_out=gsum[:, :]).then_inc(S["gexp_ready"], 1)
                        tanh(r, -1, 1)
                    if j == 0 and has_pair(low + 1):
                        wait(act, "qk_done", r, lambda i: i + 2)
                        wait(act, "parts_out", r, lambda i: 16 * 6 * (i + 1))
                        for t in range(2):
                            act.activation(parts[:, 0, t, :], m_ps[:, T * t:T * t + T], ACT.Identity,
                                           bias=bqk[:, t:t + 1]).then_inc(S["part1_ready"], 1)
                    if here:
                        exp(r, j, 3)
                    if j == 0 and has_pair(low + 1):
                        wait(act, "rest_ready", r, lambda i: i + 2)
                        act.copy(parts[:, 1, :, :], rest[:, :, :]).then_inc(S["part2_ready"], 1)
                    if j == 2 and has_pair(low - 1):
                        wait(act, "combt_done", r, lambda i: i)
                        wait(act, "crow_in", r, lambda i: 16 * (i - 1))
                        act.copy(combT[:, :], m_ps[0:NE, 0:P]).then_inc(S["combt_ready"], 1)

            run(act, body)

        @block.gpsimd
        def _(pool):
            link = Link(pool, S["pool_link"])
            link(pool.memset(mhalf[:, :], -0.5))
            link.wait()

            def constants():
                link(pool.memset(ks[:, :, :, :].rearrange("p a b c -> p (a b c)").bitcast(U32), 0))
                link(pool.memset(ident[:, :], 0.0))
                link(pool.memset(identb[:, :], 0.0))
                link(pool.memset(band[:, :, :], 0.0))
                link.wait()
                pool.memset(ks[MROW:MROW + PARTS, :, :, :], 1.0).then_inc(S["ks_ready"], 1)
                pool.wait_ge(S["ks_ready"], 1)
                for sign in (1, -1):
                    for t in range(2):
                        link(pool.affine_select(out=band[:, t, :], in_=band[:, t, :], compare_op=ALU.is_ge, fill=NEG,
                                                base=BAND + sign * (BAND - P) * t, pattern=[[sign, W]],
                                                channel_multiplier=-sign))
                    link.wait()
                for t in (ident, identb):
                    pool.affine_select(out=t[:, :], in_=t[:, :], compare_op=ALU.not_equal, fill=1.0, base=0,
                                       pattern=[[-1, P]], channel_multiplier=1).then_inc(S["ident_ready"], 1)

            def rstd(r, ready, ve, rs, done, p):
                wait(pool, ready, r, lambda i: i + p + 1)
                pool.tensor_tensor(rs[:, :], ve[:, :], mhalf[:, :], ALU.pow).then_inc(S[done], 1)

            def band_cut(r, j, kt):
                wait(pool, "exp_done", r, lambda i: 4 * (4 * i + j) + 2 * kt + 2, alone=True)
                edge = BAND * (1 + kt)
                low_side = pt[:, j % 2, kt, :, 0:edge]
                high_side = pt[:, j % 2, kt, :, edge:W]
                pool.affine_select(out=low_side, in_=low_side, compare_op=ALU.is_ge, fill=0.0,
                                   base=BAND - BAND * kt, pattern=[[0, HG], [1, edge]],
                                   channel_multiplier=-1).then_inc(S["band_done"], 1)
                pool.affine_select(out=high_side, in_=high_side, compare_op=ALU.is_ge, fill=0.0,
                                   base=BAND + BAND * kt - edge, pattern=[[0, HG], [-1, W - edge]],
                                   channel_multiplier=1).then_inc(S["band_done"], 1)

            def weigh(r, o, s):
                e0 = experts_of(s)[0]
                if s == 1:
                    wait(pool, "crow_in", r, lambda i: 16 * (i + o + 1), alone=True)
                    pool.partition_broadcast(cb[:, :], crow[:, :], P).then_inc(S["cb_ready"], 1)
                    wait(pool, "cb_ready", r, lambda i: i + o + 1)
                wait(pool, "hidden_ready", r, lambda i: SLOTS * (i + o) + s + 1)
                wait(pool, "down_done", r, lambda i: SLOTS * (i + o) + s - 1)
                pool.tensor_tensor(gwt[:, s % 2, :, :].rearrange("p e t -> p (e t)"), g[:, s % 2, :],
                                   cb[:, e0 * P:(e0 + 2) * P], ALU.mult).then_inc(S["gated_ready"], 1)

            def body(r):
                i, low = r
                for j in range(4):
                    if j == 0 and has_pair(low + 1):
                        rstd(r, "ve1_ready", ve1, rs1, "rs1_ready", 1)
                    if j == 0 and low == -1:
                        constants()
                    if j in (0, 1):
                        for o, s in slots_in(low, j):
                            weigh(r, o, s)
                    if j == 1 and has_pair(low - 1):
                        rstd(r, "ve2_ready", ve2, rs2, "rs2_ready", -1)
                    if has_half(4 * low + j):
                        band_cut(r, j, 0)
                    if j == 3:
                        for o, s in [(-1, 1)] * has_pair(low - 1) + slots_in(low, j):
                            weigh(r, o, s)
                    if has_half(4 * low + j):
                        band_cut(r, j, 1)

            run(pool, body)

        @block.vector
        def _(dve):
            link = Link(dve, S["dve_link"])
            dve.memset(wqk[:, :, :], 0.0).then_inc(S["zeros_ready"], 1)
            dve.memset(wv[:, :], 0.0).then_inc(S["zeros_ready"], 1)
            dve.memset(wo[:, :, :], 0.0).then_inc(S["zeros_ready"], 1)
            dve.memset(wct[:, :], 0.0).then_inc(S["zeros_ready"], 1)
            dve.memset(zrows[:, :].bitcast(U32), 0).then_inc(S["zeros_ready"], 1)

            def norm_stats(src, stat, mv, ve, ready):
                link(dve.bn_stats(stat[:, :], src[:, :]))
                link.wait(hold)
                link(dve.bn_aggr(mv[:, :], stat[:, :]))
                link.wait()
                dve.tensor_scalar(ve[:, :], mv[:, 1:2], EPS, None, ALU.add).then_inc(S[ready], 1)

            def row_max(r, j, n):
                qt = n // 2
                if n == 0:
                    wait(dve, "mt_done", r, lambda i: 4 * i + j + 1)
                wait(dve, "s_done", r, lambda i: 4 * (4 * i + j + 2) + n + 1, alone=True)
                for hd in range(2):
                    col = 2 * (2 * (n % 2) + hd) + qt
                    ins = dve.tensor_tensor_reduce(masked[:, 2 * n + hd, :], s_ps[:, n % 2, W * hd:W * hd + W], band[:, qt, :], 1.0, NEG,
                                                   ALU.add, ALU.max, mx[:, j % 2, col:col + 1])
                ins.then_inc(S["max_done"], 1)

            def max_parts(r, j):
                m, part = mx[:, j % 2, :], mparts[:, j % 2, :, :]
                wait(dve, "max_done", r, lambda i: 4 * (4 * i + j + 3))
                link(dve.tensor_scalar(part[:, 0, :], m, -1.0, None, ALU.mult))
                link.wait()
                link(dve.scalar_tensor_tensor(out=mrest[:, :], in0=m, scalar=-1.0, in1=part[:, 0, :],
                                              op0=ALU.mult, op1=ALU.subtract))
                link.wait()
                link(dve.tensor_copy(part[:, 1, :], mrest[:, :]))
                link.wait()
                dve.tensor_tensor(part[:, 2, :], mrest[:, :], part[:, 1, :], ALU.subtract).then_inc(S["mparts_ready"], 1)

            def divide(r, b, p):
                wait(dve, "pv_done", r, lambda i: 4 * (i + p) + 2 * b + 2)
                ins = dve.transpose(o1[:, :, :].rearrange("p a b -> p (a b)"), pv_ps[:, :])
                ins.then_inc(S["pv_read"], 1)
                wait(dve, "pv_read", r, lambda i: 2 * (i + p) + b + 1)
                link(dve.reciprocal(rden[:, :], o1[:, :, D]))
                link.wait()
                link(dve.tensor_tensor(o2[:, :, 0:D], o1[:, :, 0:D], rden[:, :].unsqueeze(2).to_broadcast([P, 16, D]), ALU.mult))
                link.wait()
                wait(dve, "o_done", r, lambda i: i + p)
                dve.transpose(oT[:, b, :], o2[:, :, :].rearrange("p a b -> p (a b)")).then_inc(S["oT_ready"], 1)

            def hidden(r, o, s):
                n = len(experts_of(s)) * P
                wait(dve, "tanh_done", r, lambda i: SLOTS * (i + o) + s + 1)
                link(dve.scalar_tensor_tensor(out=u[:, 0:n], in0=th[:, 0:n], scalar=1.0, in1=h_ps[:, 0:n],
                                              op0=ALU.add, op1=ALU.mult))
                link.wait()
                if s == 0:
                    wait(dve, "down_done", r, lambda i: SLOTS * (i + o))
                    dst = gwt[:, 0, 0, :]
                else:
                    wait(dve, "gated_ready", r, lambda i: 4 * (i + o) + max(s - 2, 0))
                    dst = g[:, s % 2, 0:n]
                dve.scalar_tensor_tensor(out=dst, in0=u[:, 0:n], scalar=0.5, in1=h_ps[:, 2 * P:2 * P + n],
                                         op0=ALU.mult, op1=ALU.mult).then_inc(S["hidden_ready"], 1)

            def body(r):
                i, low = r
                for j in range(4):
                    ahead = has_half(4 * low + j + 2)
                    slots = slots_in(low, j)
                    if ahead:
                        row_max(r, j, 0)
                    if j == 0:
                        if has_pair(low + 1):
                            wait(dve, "x_in", r, lambda i: 16 * (i + 2))
                            norm_stats(xin, stat1, mv1, ve1, "ve1_ready")
                        if has_pair(low):
                            wait(dve, "v_done", r, lambda i: i + 1)
                            wait(dve, "pv_done", r, lambda i: 4 * i)
                            if low == 0:
                                dve.wait_ge(S["w_v_in"], 16 * 6)
                            dve.tensor_tensor(v[:, :, :, :, 0:D].rearrange("p a b h d -> p (a b h) d"),
                                              m_ps[:, 0:2 * P].rearrange("p (a d) -> p a d", d=D),
                                              bv[:, :, :].rearrange("p a (h d) -> p (a h) d", d=D),
                                              ALU.add).then_inc(S["v_ready"], 1)
                        if has_pair(low + 1):
                            wait(dve, "rs1_ready", r, lambda i: i + 2)
                            wait(dve, "v_done", r, lambda i: i + 1)
                            dve.tensor_scalar(xn[:, :], xin[:, :], mv1[:, 0:1], rs1[:, 0:1], ALU.subtract,
                                              ALU.mult).then_inc(S["xn_ready"], 1)
                        if low == -1:
                            dve.memset(qs[:, :, :, :].rearrange("p a b c -> p (a b c)").bitcast(U32), 0).then_inc(S["zeros_ready"], 1)
                            dve.memset(v[:, :, :, :, :], 1.0).then_inc(S["consts_ready"], 1)
                            dve.memset(o2[:, :, :], 1.0).then_inc(S["consts_ready"], 1)
                            for e in range(NE):
                                dve.memset(iota8[:, e:e + 1], float(e)).then_inc(S["consts_ready"], 1)
                            dve.wait_ge(S["consts_ready"], 2 + NE)
                            dve.wait_ge(S["ident_ready"], 2)
                            dve.wait_ge(S["w_qk_in"], 16 * 8)
                    if j in (0, 1):
                        for o, s in slots:
                            hidden(r, o, s)
                    if j == 3 and has_pair(low):
                        divide(r, 0, 0)
                    if ahead:
                        row_max(r, j, 1)
                    if j == 0 and has_pair(low - 1):
                        divide(r, 1, -1)
                    if j == 1 and has_pair(low - 1):
                        wait(dve, "o_done", r, lambda i: i)
                        wait(dve, "ctx_in", r, lambda i: 32 * i)
                        wait(dve, "ct_done", r, lambda i: i - 1)
                        dve.scalar_tensor_tensor(out=y[:, :], in0=m_ps[:, 0:T], scalar=0.0, in1=ctx[:, :],
                                                 op0=ALU.max, op1=ALU.mult).then_inc(S["y_ready"], 1)
                    if j == 1 and has_pair(low - 2):
                        wait(dve, "down_done", r, lambda i: SLOTS * (i - 1))
                        wait(dve, "out_done", r, lambda i: 16 * (i - 2))
                        dve.tensor_tensor(res[:, :], y_ps[:, 0:T], x2[:, :], ALU.add).then_inc(S["res_ready"], 1)
                    if j == 1 and has_pair(low - 1):
                        wait(dve, "res_ready", r, lambda i: i - 1)
                        wait(dve, "ct_done", r, lambda i: i)
                        if low == 1:
                            dve.wait_ge(S["w_ct_in"], 16 * 4)
                        dve.scalar_tensor_tensor(out=x2[:, :], in0=m_ps[:, 0:T], scalar=bct[:, 0:1], in1=xres[:, :],
                                                 op0=ALU.add, op1=ALU.add).then_inc(S["x2_ready"], 1)
                        wait(dve, "x2_ready", r, lambda i: i)
                        norm_stats(x2, stat2, mv2, ve2, "ve2_ready")
                    if j == 2 and has_pair(low - 1):
                        hidden(r, -1, 0)
                    if ahead:
                        row_max(r, j, 2)
                    if j == 1 and has_pair(low - 1):
                        wait(dve, "rs2_ready", r, lambda i: i)
                        wait(dve, "xt_done", r, lambda i: i - 1)
                        dve.tensor_scalar(xn2[:, :], x2[:, :], mv2[:, 0:1], rs2[:, 0:1], ALU.subtract,
                                          ALU.mult).then_inc(S["xn2_ready"], 1)
                    if j == 2 and has_pair(low - 1):
                        wait(dve, "g_done", r, lambda i: i, alone=True)
                        link(dve.max(gtop[:, :], m_ps[:, 0:NE]))
                        link.wait()
                        dve.tensor_scalar(gdif[:, :], m_ps[:, 0:NE], gtop[:, 0:1], None,
                                          ALU.subtract).then_inc(S["gdif_ready"], 1)
                    if j == 0 and has_pair(low + 1):
                        wait(dve, "part1_ready", r, lambda i: 2 * (i + 2))
                        for t in range(2):
                            ins = dve.scalar_tensor_tensor(out=rest[:, t, :], in0=m_ps[:, T * t:T * t + T],
                                                           scalar=bqk[:, t:t + 1], in1=parts[:, 0, t, :],
                                                           op0=ALU.add, op1=ALU.subtract)
                        ins.then_inc(S["rest_ready"], 1)
                    if j == 3:
                        for o, s in slots:
                            hidden(r, o, s)
                    if ahead:
                        row_max(r, j, 3)
                        max_parts(r, j)
                    if j == 0 and has_pair(low + 1):
                        wait(dve, "part2_ready", r, lambda i: i + 2)
                        wait(dve, "parts_out", r, lambda i: 16 * 6 * (i + 1))
                        dve.tensor_tensor(parts[:, 2, :, :], rest[:, :, :], parts[:, 1, :, :],
                                          ALU.subtract).then_inc(S["parts_ready"], 1)
                    if j == 2 and has_pair(low - 1):
                        wait(dve, "gexp_ready", r, lambda i: i)
                        link(dve.reciprocal(grec[:, :], gsum[:, :]))
                        link.wait()
                        link(dve.tensor_scalar(prob[:, :], gexp[:, :], grec[:, 0:1], None, ALU.mult))
                        link.wait(hold)
                        link(dve.max(ptop[:, :], prob[:, :]))
                        link.wait(hold)
                        link(dve.max_index(pidx[:, :], ptop[:, :], prob[:, :]))
                        link.wait()
                        link(dve.tensor_copy(pidf[:, :], pidx[:, 0:2]))
                        link.wait()
                        for n in range(2):
                            link(dve.tensor_scalar(pick[:, n, :], iota8[:, :], pidf[:, n:n + 1], ptop[:, n:n + 1],
                                                   ALU.is_equal, ALU.mult))
                        link.wait()
                        wait(dve, "combt_done", r, lambda i: i - 1)
                        dve.tensor_tensor(comb[:, :], pick[:, 0, :], pick[:, 1, :], ALU.add).then_inc(S["comb_ready"], 1)
                        hidden(r, -1, 1)

            run(dve, body, link, DVE_LINKS)

        @block.tensor
        def _(pe):
            def scores(r, j, n):
                slot, qt, g0 = (j + 2) % 4, n // 2, 2 * (n % 2)
                if n == 0:
                    wait(pe, loaded[slot], r, lambda i: 16 * LOADS * (i + (j + 2) // 4 + 1))
                wait(pe, "max_done", r, lambda i: 4 * (4 * i + j + 2) + n - 1)
                for hd in range(2):
                    ins = pe.matmul(s_ps[:, n % 2, W * hd:W * hd + W], qs[:, slot, g0 + hd, P * qt:P * qt + P],
                                    ks[:, slot, g0 + hd, BAND * qt:BAND * qt + W], start=True, stop=True)
                ins.then_inc(S["s_done"], 1)

            def scores_t(r, j, n):
                kt, g0 = n // 2, 2 * (n % 2)
                if n == 0:
                    wait(pe, "row_in", r, lambda i: 16 * PARTS * (4 * i + j + 1))
                wait(pe, "exp_done", r, lambda i: 4 * (4 * i + j) + n - 1)
                for hd in range(2):
                    ins = pe.matmul(st_ps[:, n % 2, W * hd:W * hd + W], ks[:, j, g0 + hd, P * kt:P * kt + P],
                                    qs[:, j, g0 + hd, BAND * kt:BAND * kt + W], start=True, stop=True)
                ins.then_inc(S["st_done"], 1)

            def turn_max(r, j):
                wait(pe, "mparts_ready", r, lambda i: 4 * i + j + 2)
                free_misc(r, j, "mt")
                pe.matmul(m_ps[0:PARTS * 2 * HG, 0:P], mparts[:, (j + 1) % 2, :, :].rearrange("p a b -> p (a b)"), identb[:, :],
                          start=True, stop=True).then_inc(S["mt_done"], 1)

            def free_misc(r, j, use):
                def last(s, f):
                    wait(pe, s, r, f)
                if use == "mt":
                    last("mt_ready", lambda i: 4 * i + j + 1)
                    if j == 1:
                        last("part1_ready", lambda i: 2 * (i + 2) if has_pair(r[1] + 1) else 0)
                        last("rest_ready", lambda i: i + 2 if has_pair(r[1] + 1) else 0)
                    if j == 0:
                        last("v_ready", lambda i: i)
                    if j == 2:
                        last("x2_ready", lambda i: i if has_pair(r[1] - 1) else 0)
                    if j == 3:
                        last("combt_ready", lambda i: i if has_pair(r[1] - 1) else 0)
                elif use == "first":
                    if has_half(4 * r[1] + j + 1):
                        last("mt_ready", lambda i: 4 * i + j + 2)

            def probs_v(r, j, kt):
                slot = (j - 1) % 4
                b, hh = slot // 2, slot % 2
                wait(pe, "band_done", r, lambda i: 4 * (4 * i + j - 1) + 2 * kt + 2)
                if kt == 0:
                    wait(pe, "v_ready", r, lambda i: i + (j + 3) // 4)
                    if hh == 0:
                        wait(pe, "pv_read", r, lambda i: (4 * i + j - 1) // 2 if isinstance(i, int) else 2 * i + (j - 1) // 2)
                for gq in range(HG):
                    ins = pe.matmul(pv_ps[32 * gq:32 * gq + 32, T * hh + BAND * kt:T * hh + BAND * kt + W],
                                    v[:, kt, b, HG * hh + gq, :], pt[:, (j - 1) % 2, kt, gq, :],
                                    start=(kt == 0), stop=(kt == 1), skip_group_check=True)
                if kt == 1:
                    ins.then_inc(S["pv_done"], 1)

            def up(r, o, s):
                es = experts_of(s)
                wait(pe, "hidden_ready", r, lambda i: SLOTS * (i + o) + s)
                if s == 0:
                    wait(pe, "xt_ready", r, lambda i: i + o + 1)
                    if r[1] + o == 0:
                        pe.wait_ge(S["w_ffn_in"], 16 * 6)
                for t, w in enumerate((w1, w3)):
                    for n, e in enumerate(es):
                        c0 = (2 * t + n) * P
                        for c in range(2):
                            ins = pe.matmul(h_ps[:, c0:c0 + P], w[:, c, e * INTER:(e + 1) * INTER], xn2T[:, c, :],
                                            start=(c == 0), stop=(c == 1))
                ins.then_inc(S["up_done"], 1)

            def down(r, o, s):
                es = experts_of(s)
                if s == 0:
                    wait(pe, "hidden_ready", r, lambda i: SLOTS * (i + o) + 1)
                    wait(pe, "res_ready", r, lambda i: i + o)
                else:
                    wait(pe, "gated_ready", r, lambda i: 4 * (i + o) + s)
                for n, e in enumerate(es):
                    ins = pe.matmul(y_ps[:, 0:T], gwt[:, s % 2, n, :], w2[:, e, :],
                                    start=(s == 0), stop=(s == SLOTS - 1 and n == 1))
                ins.then_inc(S["down_done"], 1)

            def body(r):
                i, low = r
                for j in range(4):
                    here, ahead, rows, back = (has_half(4 * low + j + d) for d in (0, 2, 1, -1))
                    mid = has_pair(low - 1)

                    def unit(n):
                        if here:
                            scores_t(r, j, n)
                        if ahead:
                            scores(r, j, n)

                    unit(0)
                    if rows:
                        turn_max(r, j)
                    if j == 0:
                        if back:
                            probs_v(r, 0, 0)
                            probs_v(r, 0, 1)
                        if has_pair(low):
                            free_misc(r, j, "first")
                            if low == 0:
                                pe.wait_ge(S["w_v_in"], 16 * 6)
                            for kt in range(2):
                                ins = pe.matmul(m_ps[:, P * kt:P * kt + P], xn[:, P * kt:P * kt + P], wv[:, :],
                                                start=True, stop=True)
                            ins.then_inc(S["v_done"], 1)
                        for o, s in slots_in(low, j):
                            up(r, o, s)
                        unit(1)
                        unit(2)
                        for o, s in slots_in(low, j):
                            down(r, o, s)
                        if has_pair(low + 1):
                            wait(pe, "xn_ready", r, lambda i: i + 2)
                            wait(pe, "v_ready", r, lambda i: i + 1)
                            if low == -1:
                                pe.wait_ge(S["w_qk_in"], 16 * 8)
                            for t in range(2):
                                ins = pe.matmul(m_ps[:, T * t:T * t + T], wqk[:, t, :], xn[:, :], start=True, stop=True)
                            ins.then_inc(S["qk_done"], 1)
                        unit(3)
                    if j == 1:
                        for o, s in slots_in(low, j):
                            up(r, o, s)
                        if mid:
                            free_misc(r, j, "first")
                            wait(pe, "oT_ready", r, lambda i: 2 * i)
                            if not rows:
                                wait(pe, "mt_ready", r, lambda i: 4 * PAIRS)
                            if low == 1:
                                pe.wait_ge(S["w_o_in"], 16 * 9)
                            for b in range(2):
                                for hh in range(2):
                                    ins = pe.matmul(m_ps[C * b:C * b + C, 0:T], wo[:, hh, :], oT[:, b, T * hh:T * hh + T],
                                                    start=(hh == 0), stop=(hh == 1))
                            ins.then_inc(S["o_done"], 1)
                        unit(1)
                        if back:
                            probs_v(r, j, 0)
                            probs_v(r, j, 1)
                        for o, s in slots_in(low, j):
                            down(r, o, s)
                        if mid:
                            wait(pe, "y_ready", r, lambda i: i)
                            if low == 1:
                                pe.wait_ge(S["w_ct_in"], 16 * 4)
                            pe.matmul(m_ps[:, 0:T], wct[:, :], y[:, :], start=True, stop=True).then_inc(S["ct_done"], 1)
                        unit(2)
                        unit(3)
                    if j == 2:
                        if mid:
                            free_misc(r, j, "first")
                            wait(pe, "xn2_ready", r, lambda i: i)
                            for c in range(2):
                                ins = pe.transpose(m_ps[:, P * c:P * c + P], xn2[:, P * c:P * c + P], ident[:, :])
                            ins.then_inc(S["xt_done"], 1)
                        if back:
                            probs_v(r, j, 0)
                            probs_v(r, j, 1)
                        unit(1)
                        if mid:
                            wait(pe, "xt_ready", r, lambda i: i)
                            if low == 1:
                                pe.wait_ge(S["w_gate_in"], 16)
                            for c in range(2):
                                ins = pe.matmul(m_ps[0:NE, 0:P], gw[:, c, :], xn2T[:, c, :], start=(c == 0), stop=(c == 1))
                            ins.then_inc(S["gt_done"], 1)
                            up(r, -1, 0)
                            wait(pe, "gt_ready", r, lambda i: i, alone=True)
                            pe.transpose(m_ps[:, 0:NE], gT[:, :], ident[0:NE, 0:NE]).then_inc(S["g_done"], 1)
                        unit(2)
                        if mid:
                            down(r, -1, 0)
                            up(r, -1, 1)
                        unit(3)
                        if mid:
                            wait(pe, "comb_ready", r, lambda i: i)
                            pe.transpose(m_ps[0:NE, 0:P], comb[:, :], ident[:, :]).then_inc(S["combt_done"], 1)
                    if j == 3:
                        unit(1)
                        if mid:
                            down(r, -1, 1)
                            up(r, -1, 2)
                        if back:
                            probs_v(r, j, 0)
                            probs_v(r, j, 1)
                        unit(2)
                        unit(3)
                        if mid:
                            down(r, -1, 2)

            pe.wait_ge(S["ident_ready"], 2)
            run(pe, body)


DVE_LINKS = 33

_IN = ["x", "ctx_in", "w_qkT", "b_qk", "w_vT", "b_v", "w_oT", "b_o", "w_ct", "b_ct", "gate_wT", "w1T", "w3T", "w2T",
       "ws1T", "ws3T", "ws2T"]


def kernel(x, ctx_2048, L0_xattn_w_in, L0_xattn_b_in, L0_xattn_w_out, L0_xattn_b_out, L0_xattn_w_ct, L0_xattn_b_ct,
           L0_ffn_gate_w, L0_ffn_w1, L0_ffn_w2, L0_ffn_w3, L0_ffn_ws1, L0_ffn_ws2, L0_ffn_ws3):
    import numpy as np
    import concourse.bacc as bacc
    from concourse.bass_utils import run_bass_kernel_spmd

    a = {k: np.asarray(t) for k, t in locals().items() if k not in ("np", "bacc", "run_bass_kernel_spmd")}
    w_in, b_in = a["L0_xattn_w_in"], a["L0_xattn_b_in"]
    w_qk = w_in[:2 * C].reshape(2, H, D, C).transpose(3, 0, 2, 1).reshape(C, 2 * C)
    b_qk = b_in[:2 * C].reshape(2, H, D).transpose(0, 2, 1).reshape(2 * C, 1)
    ins = {
        "x": a["x"].reshape(B * C, T), "ctx_in": a["ctx_2048"].reshape(B * C, T),
        "w_qkT": w_qk, "b_qk": b_qk,
        "w_vT": w_in[2 * C:].T, "b_v": b_in[2 * C:].reshape(1, C),
        "w_oT": a["L0_xattn_w_out"].T, "b_o": a["L0_xattn_b_out"].reshape(1, C),
        "w_ct": a["L0_xattn_w_ct"], "b_ct": a["L0_xattn_b_ct"].reshape(C, 1),
        "gate_wT": a["L0_ffn_gate_w"].T,
        "w1T": a["L0_ffn_w1"].transpose(2, 0, 1).reshape(T, NE * INTER),
        "w3T": a["L0_ffn_w3"].transpose(2, 0, 1).reshape(T, NE * INTER),
        "w2T": a["L0_ffn_w2"].transpose(2, 0, 1),
        "ws1T": a["L0_ffn_ws1"].T, "ws3T": a["L0_ffn_ws3"].T, "ws2T": a["L0_ffn_ws2"].T,
    }
    nc = bacc.Bacc("TRN2", target_bir_lowering=False, num_devices=1)
    arrays, args = {}, []
    for name in _IN:
        t = np.ascontiguousarray(ins[name])
        arrays[f"in_{name}"] = t
        args.append(nc.dram_tensor(f"in_{name}", t.shape, mybir.dt.from_np(t.dtype), kind="ExternalInput").ap())
    args.append(nc.dram_tensor("out_0", (B * C, T), F32, kind="ExternalOutput").ap())
    build(nc, *args)
    r = run_bass_kernel_spmd(nc, [arrays], core_ids=[0])
    return r.results[0]["out_0"].reshape(B, C, T)
```

```python
from contextlib import ExitStack

import concourse.bass as bass
from concourse import mybir

F32 = mybir.dt.float32
BF16 = mybir.dt.bfloat16
U32 = mybir.dt.uint32
ALU = mybir.AluOpType
ACT = mybir.ActivationFunctionType

P = 128
B, C, T = 16, 64, 256
PAIRS = B * C // P
HALVES = 4 * PAIRS
H, D = 8, 8
HG = 4
BAND = 64
W = P + BAND
NE, INTER = 8, 128
PARTS = 3
SPAN = PARTS * D
MROW = 96
EPS = 1e-5
NEG = -3.0e38
SLOTS = 5
LOADS = 3
TURNS = 2 * PARTS - 1
LOOP_LO, LOOP_HI = 2, PAIRS - 2


def experts_of(s):
    return [NE] if s == 0 else [2 * s - 2, 2 * s - 1]


class Link:

    def __init__(self, eng, sem):
        self.eng, self.sem, self.base, self.n = eng, sem, 0, 0

    def __call__(self, ins):
        self.n += 1
        ins.then_inc(self.sem, 1)
        return self.n

    def wait(self, n=None, wait_ge=None):
        (wait_ge or type(self.eng).wait_ge)(self.eng, self.sem, self.base + (n or self.n))

    def enter(self, i, per):
        self.start, self.per = self.base + self.n, per
        self.base, self.n = (i - LOOP_LO) * per + self.start, 0

    def leave(self):
        assert self.n == self.per, f"{self.n} links in an iteration"
        self.base, self.n = self.start + (LOOP_HI - LOOP_LO) * self.per, 0


HELD = {mybir.EngineType.SP: "sync", mybir.EngineType.Pool: "pool", mybir.EngineType.DVE: "vector", mybir.EngineType.PE: "tensor",
        mybir.EngineType.Activation: "scalar"}


def build(nc, x, ctx_in, w_qkT, b_qk, w_vT, b_v, w_oT, b_o, w_ct, b_ct, gate_wT, w1T, w3T, w2T, ws1T, ws3T, ws2T, out):
    with ExitStack() as st:
        def sb(name, shape, dt=F32):
            return st.enter_context(nc.sbuf_tensor(name, shape, dt))

        def ps(name, shape):
            return st.enter_context(nc.psum_tensor(name, shape, F32))

        def sem(name):
            return st.enter_context(nc.semaphore(name))

        s_ps = ps("s_ps", [P, 2, 512])
        st_ps = ps("st_ps", [P, 2, 512])
        h_ps = ps("h_ps", [P, 512])
        y_ps = ps("y_ps", [P, 512])
        pv_ps = ps("pv_ps", [P, 512])
        m_ps = ps("m_ps", [P, 512])

        q_dram = nc.dram_tensor("q_parts", (2, PARTS, D * H, T), BF16, kind="Internal").ap()
        k_dram = nc.dram_tensor("k_parts", (2, TURNS, D * H, T), BF16, kind="Internal").ap()

        wqk = sb("wqk", [P, 2, P])
        bqk = sb("bqk", [P, 2])
        wv = sb("wv", [P, P])
        bv = sb("bv", [P, 2, P])
        wo = sb("wo", [P, 2, C])
        wct = sb("wct", [P, P])
        bct = sb("bct", [P, 1])
        gw = sb("gw", [P, 2, NE])
        w1 = sb("w1", [P, 2, (NE + 1) * INTER])
        w3 = sb("w3", [P, 2, (NE + 1) * INTER])
        w2 = sb("w2", [P, NE + 1, T])
        ident = sb("ident", [P, P])
        identb = sb("identb", [P, P], BF16)
        band = sb("band", [P, 2, W])
        iota8 = sb("iota8", [P, NE])
        mhalf = sb("mhalf", [P, 1])
        zrows = sb("zrows", [PARTS, HG * T], BF16)

        xin = sb("xin", [P, T])
        xn = sb("xn", [P, T])
        stat1, mv1, ve1, nm1, rs1 = sb("stat1", [P, 6]), sb("mv1", [P, 2]), sb("ve1", [P, 1]), sb("nm1", [P, 1]), sb("rs1", [P, 1])
        parts = sb("parts", [P, 2, TURNS, T], BF16)
        rest = sb("rest", [P, 2, T])
        qs = sb("qs", [P, 4, HG, T], BF16)
        ks = sb("ks", [P, 4, HG, T], BF16)
        masked = sb("masked", [P, 8, W])
        mx = sb("mx", [P, 2, 2 * HG])
        mparts = sb("mparts", [P, 2, PARTS, 2 * HG], BF16)
        mrest = sb("mrest", [P, 2 * HG])
        mt = sb("mt", [PARTS * 2 * HG, 2, P], BF16)
        pt = sb("pt", [P, 2, 2, HG, W])
        v = sb("v", [P, 2, 2, H, 32])
        vnext = sb("vnext", [P, 2, P])
        o1 = sb("o1", [P, 16, 32])
        rden = sb("rden", [P, 16])
        o2 = sb("o2", [P, 16, 32])
        oT = sb("oT", [P, 2, 2 * T])

        ctx = sb("ctx", [P, T])
        xres = sb("xres", [P, T])
        y = sb("y", [P, T])
        x2 = sb("x2", [P, T])
        x2k = sb("x2k", [P, T])
        stat2, mv2, ve2, nm2, rs2 = sb("stat2", [P, 6]), sb("mv2", [P, 2]), sb("ve2", [P, 1]), sb("nm2", [P, 1]), sb("rs2", [P, 1])
        xn2 = sb("xn2", [P, T])
        xn2T = sb("xn2T", [P, 2, P])
        gT = sb("gT", [NE, P])
        gtop, gdif, gexp, gsum, grec = (sb("gtop", [P, 8]), sb("gdif", [P, NE]), sb("gexp", [P, NE]),
                                        sb("gsum", [P, 1]), sb("grec", [P, 1]))
        prob, ptop, pidx, pidf = sb("prob", [P, NE]), sb("ptop", [P, 8]), sb("pidx", [P, 8], U32), sb("pidf", [P, 2])
        pick, comb, combT, crow, cb = (sb("pick", [P, 2, NE]), sb("comb", [P, NE]), sb("combT", [NE, P]),
                                       sb("crow", [1, NE * P]), sb("cb", [P, NE * P]))
        th, u, g = sb("th", [P, 2 * P]), sb("u", [P, 2 * P]), sb("g", [P, 2, 2 * P])
        gwt = sb("gwt", [P, 2, 2, P])
        res = sb("res", [P, T])

        NAMES = """x_in ctx_in w_qk_in w_v_in w_o_in w_ct_in w_gate_in w_ffn_in parts_out row_in crow_in out_done
            consts_ready head_ready mrest_ready mid_ready dup_ready x2k_ready zeros_ready ident_ready ks_ready
            ve1_ready rs1_ready xn_ready v_done vnext_ready v_ready qk_done part1_ready rest_ready part2_ready parts_ready
            s_done max_done mparts_ready mt_done mt_ready st_done exp_done band_done pv_done pv_read
            oT_ready o_done y_ready ct_done x2_ready ve2_ready rs2_ready xn2_ready xt_done xt_ready
            gt_done gt_ready g_done gdif_ready gexp_ready comb_ready combt_done combt_ready cb_ready
            up_done tanh_done hidden_ready gated_ready down_done res_ready dve_link pool_link held_sync held_pool held_vector held_tensor held_scalar""".split()
        S = {n: sem(n) for n in NAMES}
        loaded = [sem(f"loaded{j}") for j in range(4)]

        def hold(eng, sem, value):
            eng.wait_ge(sem, value).then_inc(S["held_" + HELD[eng.engine]], 1)

        def wait(eng, s, r, value, alone=False):
            i, low = r
            if value(low) > 0:
                (hold if alone or eng.engine == mybir.EngineType.SP else type(eng).wait_ge)(eng, S[s] if isinstance(s, str) else s, value(i))

        def run(eng, body, link=None, per=0):
            for i in range(-1, LOOP_LO):
                body((i, i))
            with eng.Fori(LOOP_LO, LOOP_HI) as i:
                if link:
                    link.enter(i, per)
                body((i, LOOP_LO))
                if link:
                    link.leave()
            for i in range(LOOP_HI, PAIRS + 2):
                body((i, i))

        def has_half(k):
            return 0 <= k < HALVES

        def has_pair(p):
            return 0 <= p < PAIRS

        block = st.enter_context(nc.Block())

        @block.sync
        def _(sp):
            sp.dma_start(xin[:, :], x[0:P, :]).then_inc(S["x_in"], 16)
            sp.wait_ge(S["zeros_ready"], 2)
            for b in range(2):
                c = slice(C * b, C * b + C)
                for t in range(2):
                    sp.dma_start(wqk[c, t, c], w_qkT[:, C * t:C * t + C]).then_inc(S["w_qk_in"], 16)
                    sp.dma_start(bqk[c, t:t + 1], b_qk[C * t:C * t + C, :]).then_inc(S["w_qk_in"], 16)
            for b in range(2):
                c = slice(C * b, C * b + C)
                sp.dma_start(wv[c, c], w_vT).then_inc(S["w_v_in"], 16)
                for kt in range(2):
                    sp.dma_start(bv[:, kt, c], b_v.to_broadcast([P, C])).then_inc(S["w_v_in"], 16)

            def stacks(i, low, off):
                slot = off % 4
                b, hh = slot // 2, slot % 2
                pair = (i + off // 4, low + off // 4)
                wait(sp, "st_done", (i, low), lambda i: 4 * (4 * i + off - 4 + 1))
                wait(sp, "parts_out", pair, lambda p: 16 * 4 * (p + 1))
                if pair[1] == 0:
                    sp.wait_ge(S["zeros_ready"], 6)
                    sp.wait_ge(S["ks_ready"], 1)
                for dst, src, turn in ((qs, q_dram, 0), (ks, k_dram, D)):
                    v0 = src[b].rearrange("a (d h) t -> (a d) (h t)", h=H)[0:SPAN, HG * hh * T:HG * (hh + 1) * T]
                    three = bass.AP(tensor=v0.tensor, offset=v0.offset, ap=[[turn * H * T, PARTS], [H * T, SPAN], [1, HG * T]])
                    sp.dma_start(dst[0:PARTS * SPAN, slot, :, :].rearrange("r h t -> r (h t)"), three).then_inc(loaded[slot], 16)
                sp.dma_start(qs[MROW:MROW + PARTS, slot, :, :], zrows[:, :].rearrange("a (h t) -> a h t", h=HG)).then_inc(loaded[slot], 16)

            def body(r):
                i, low = r
                for j in range(4):
                    klow = 4 * low + j
                    if j != 1 and has_half(klow + 3):
                        stacks(i, low, j + 3)
                    if j == 1 and has_pair(low + 2):
                        wait(sp, "xn_ready", r, lambda i: i + 2)
                        sp.dma_start(xin[:, :], x[bass.ds((i + 2) * P, P), :]).then_inc(S["x_in"], 16)
                    if has_half(klow + 1):
                        off = j + 1
                        slot, par = off % 4, off % 2
                        wait(sp, "mt_ready", r, lambda i: 4 * i + off + 1)
                        dst = qs[MROW:MROW + PARTS, slot, :, :].rearrange("a h (q t) -> a (h q) t", q=2)
                        sp.dma_start(dst, mt[:, par, :]).then_inc(S["row_in"], 16)
                    if j == 1 and has_half(klow + 3):
                        stacks(i, low, j + 3)
                    if j == 2 and has_pair(low):
                        wait(sp, "x2_ready", r, lambda i: i)
                        sp.dma_start(ctx[:, :], ctx_in[bass.ds(i * P, P), :]).then_inc(S["ctx_in"], 16)
                        sp.dma_start(xres[:, :], x[bass.ds(i * P, P), :]).then_inc(S["ctx_in"], 16)
                    if j == 0 and has_pair(low + 1):
                        wait(sp, "parts_ready", r, lambda i: i + 2)
                        wait(sp, "dup_ready", r, lambda i: i + 2)
                        wait(sp, loaded[3], r, lambda i: 16 * LOADS * (i + 1))
                        for b in range(2):
                            for t, (dram, n) in enumerate(((q_dram, PARTS), (k_dram, TURNS))):
                                sp.dma_start(dram[b].rearrange("a r t -> r a t"),
                                             parts[C * b:C * b + C, t, 0:n, :]).then_inc(S["parts_out"], 16)
                    if j == 2 and has_pair(low - 2):
                        wait(sp, "res_ready", r, lambda i: i - 1)
                        sp.dma_start(out[bass.ds((i - 2) * P, P), :], res[:, :]).then_inc(S["out_done"], 16)
                    if j == 3 and has_pair(low - 1):
                        wait(sp, "combt_ready", r, lambda i: i)
                        wait(sp, "cb_ready", r, lambda i: i - 1)
                        sp.dma_start(crow[:, :].rearrange("a (e t) -> a e t", e=NE), combT[:, :]).then_inc(S["crow_in"], 16)

            run(sp, body)
            sp.wait_ge(S["out_done"], 16 * PAIRS)

        @block.scalar
        def _(act):
            act.wait_ge(S["zeros_ready"], 4)
            for h in range(H):
                act.dma_start(wo[32 * (h % HG):32 * (h % HG) + D, h // HG, :], w_oT[D * h:D * h + D, :]).then_inc(S["w_o_in"], 16)
            act.dma_start(wo[D:D + 1, 0, :], b_o).then_inc(S["w_o_in"], 16)
            for b in range(2):
                c = slice(C * b, C * b + C)
                act.dma_start(wct[c, c], w_ct).then_inc(S["w_ct_in"], 16)
                act.dma_start(bct[c, :], b_ct).then_inc(S["w_ct_in"], 16)
            act.dma_start(gw[:, :, :], gate_wT.rearrange("(c p) e -> p c e", p=P)).then_inc(S["w_gate_in"], 16)
            for w_sb, big, shared in ((w1, w1T, ws1T), (w3, w3T, ws3T)):
                act.dma_start(w_sb[:, :, 0:NE * INTER], big.rearrange("(c p) e -> p c e", p=P)).then_inc(S["w_ffn_in"], 16)
                act.dma_start(w_sb[:, :, NE * INTER:], shared.rearrange("(c p) e -> p c e", p=P)).then_inc(S["w_ffn_in"], 16)
            act.dma_start(w2[:, 0:NE, :], w2T).then_inc(S["w_ffn_in"], 16)
            act.dma_start(w2[:, NE, :], ws2T).then_inc(S["w_ffn_in"], 16)

            def exp(r, j, n):
                i, low = r
                kt, g0 = n // 2, 2 * (n % 2)
                wait(act, "st_done", r, lambda i: 4 * (4 * i + j) + n + 1)
                if n == 0:
                    wait(act, "pv_done", r, lambda i: 4 * i + j - 1)
                act.activation(pt[:, j % 2, kt, g0:g0 + 2, :], st_ps[:, n % 2, 0:2 * W].rearrange("p (h w) -> p h w", h=2),
                               ACT.Exp, scale=float(D) ** -0.5).then_inc(S["exp_done"], 1)

            def max_rows(r, j):
                wait(act, "mt_done", r, lambda i: 4 * i + j + 2)
                if has_half(4 * r[1] + j):
                    wait(act, "st_done", r, lambda i: 4 * (4 * i + j) + 1)
                wait(act, "row_in", r, lambda i: 16 * (4 * i + j))
                act.copy(mt[:, (j + 1) % 2, :], st_ps[0:PARTS * 2 * HG, 0, 2 * W:]).then_inc(S["mt_ready"], 1)

            def tanh(r, o, s):
                n = len(experts_of(s)) * P
                wait(act, "up_done", r, lambda i: SLOTS * (i + o) + s + 1)
                wait(act, "hidden_ready", r, lambda i: SLOTS * (i + o) + s)
                act.activation(th[:, 0:n], h_ps[:, 0:n], ACT.Tanh, scale=0.5).then_inc(S["tanh_done"], 1)

            def body(r):
                i, low = r
                mid, tail, new = has_pair(low - 1), has_pair(low - 2), has_pair(low + 1)
                for j in range(4):
                    here = has_half(4 * low + j)
                    if has_half(4 * low + j + 1):
                        max_rows(r, j)
                    if here:
                        exp(r, j, 0)
                    if j == 3 and mid:
                        wait(act, "gdif_ready", r, lambda i: i)
                        act.activation(gexp[:, :], gdif[:, :], ACT.Exp, accum_out=gsum[:, :]).then_inc(S["gexp_ready"], 1)
                    if j == 0 and new:
                        wait(act, "qk_done", r, lambda i: i + 2)
                        wait(act, "parts_out", r, lambda i: 16 * 4 * (i + 1))
                        for t in range(2):
                            act.activation(parts[:, t, 0, :], m_ps[:, T * t:T * t + T], ACT.Identity,
                                           bias=bqk[:, t:t + 1]).then_inc(S["part1_ready"], 1)
                    if here:
                        exp(r, j, 1)
                    if j == 0 and new:
                        wait(act, "rest_ready", r, lambda i: i + 2)
                        act.copy(parts[:, :, 1, :], rest[:, :, :]).then_inc(S["part2_ready"], 1)
                    if j == 0 and has_pair(low):
                        wait(act, "vnext_ready", r, lambda i: i + 1)
                        wait(act, "pv_done", r, lambda i: 4 * i)
                        act.copy(v[:, :, :, :, 0:D].rearrange("p a b h d -> p (a b h) d"),
                                 vnext[:, :, :].rearrange("p a (h d) -> p (a h) d", d=D)).then_inc(S["v_ready"], 1)
                    if j == 0 and tail:
                        tanh(r, -2, 3)
                    if j == 3 and mid:
                        tanh(r, -1, 1)
                    if j == 1 and tail:
                        tanh(r, -2, 4)
                    if j == 2 and mid:
                        wait(act, "xt_done", r, lambda i: i)
                        wait(act, "up_done", r, lambda i: SLOTS * (i - 1))
                        act.copy(xn2T[:, :, :].rearrange("p c t -> p (c t)"), m_ps[:, 0:2 * P]).then_inc(S["xt_ready"], 1)
                    if here:
                        exp(r, j, 2)
                    if j == 2 and mid:
                        wait(act, "gt_done", r, lambda i: i)
                        act.copy(gT[:, :], m_ps[0:NE, 0:P]).then_inc(S["gt_ready"], 1)
                        tanh(r, -1, 0)
                    if j == 3 and mid:
                        tanh(r, -1, 2)
                        wait(act, "combt_done", r, lambda i: i)
                        wait(act, "crow_in", r, lambda i: 16 * (i - 1))
                        act.copy(combT[:, :], m_ps[0:NE, 0:P]).then_inc(S["combt_ready"], 1)
                    if here:
                        exp(r, j, 3)
                    if j == 2 and mid:
                        wait(act, "x2_ready", r, lambda i: i)
                        wait(act, "res_ready", r, lambda i: i - 1)
                        act.copy(x2k[:, :], x2[:, :]).then_inc(S["x2k_ready"], 1)

            run(act, body)

        @block.gpsimd
        def _(pool):
            link = Link(pool, S["pool_link"])
            link(pool.memset(mhalf[:, :], -0.5))
            link.wait()

            def constants():
                link(pool.memset(ks[:, :, :, :].rearrange("p a b c -> p (a b c)").bitcast(U32), 0))
                link(pool.memset(ident[:, :], 0.0))
                link(pool.memset(identb[:, :], 0.0))
                link(pool.memset(band[:, :, :], 0.0))
                link.wait()
                pool.memset(ks[MROW:MROW + PARTS, :, :, :], -1.0).then_inc(S["ks_ready"], 1)
                pool.wait_ge(S["ks_ready"], 1)
                for sign in (1, -1):
                    for t in range(2):
                        link(pool.affine_select(out=band[:, t, :], in_=band[:, t, :], compare_op=ALU.is_ge, fill=NEG,
                                                base=BAND + sign * (BAND - P) * t, pattern=[[sign, W]],
                                                channel_multiplier=-sign))
                    link.wait()
                for t in (ident, identb):
                    pool.affine_select(out=t[:, :], in_=t[:, :], compare_op=ALU.not_equal, fill=1.0, base=0,
                                       pattern=[[-1, P]], channel_multiplier=1).then_inc(S["ident_ready"], 1)

            def normalize(r, p, n, src, ve, nm, rs, dst, used):
                wait(pool, f"ve{n}_ready", r, lambda i: i + p + 1)
                pool.tensor_tensor(rs[:, :], ve[:, :], mhalf[:, :], ALU.pow).then_inc(S[f"rs{n}_ready"], 1)
                wait(pool, used, r, lambda i: i + p)
                wait(pool, f"rs{n}_ready", r, lambda i: i + p + 1, alone=True)
                pool.tensor_scalar(dst[:, :], src[:, :], nm[:, 0:1], rs[:, 0:1], ALU.add,
                                   ALU.mult).then_inc(S["xn_ready" if n == 1 else "xn2_ready"], 1)

            def band_cut(r, j, kt):
                wait(pool, "exp_done", r, lambda i: 4 * (4 * i + j) + 2 * kt + 2, alone=True)
                edge = BAND * (1 + kt)
                low_side = pt[:, j % 2, kt, :, 0:edge]
                high_side = pt[:, j % 2, kt, :, edge:W]
                pool.affine_select(out=low_side, in_=low_side, compare_op=ALU.is_ge, fill=0.0,
                                   base=BAND - BAND * kt, pattern=[[0, HG], [1, edge]],
                                   channel_multiplier=-1).then_inc(S["band_done"], 1)
                pool.affine_select(out=high_side, in_=high_side, compare_op=ALU.is_ge, fill=0.0,
                                   base=BAND + BAND * kt - edge, pattern=[[0, HG], [-1, W - edge]],
                                   channel_multiplier=1).then_inc(S["band_done"], 1)

            def spread(r, o):
                wait(pool, "gated_ready", r, lambda i: 4 * (i + o))
                wait(pool, "crow_in", r, lambda i: 16 * (i + o + 1), alone=True)
                pool.partition_broadcast(cb[:, :], crow[:, :], P).then_inc(S["cb_ready"], 1)

            def weigh(r, o, s):
                e0 = experts_of(s)[0]
                if s == 1:
                    wait(pool, "cb_ready", r, lambda i: i + o + 1)
                wait(pool, "hidden_ready", r, lambda i: SLOTS * (i + o) + s + 1)
                wait(pool, "down_done", r, lambda i: SLOTS * (i + o) + s - 1)
                pool.tensor_tensor(gwt[:, s % 2, :, :].rearrange("p e t -> p (e t)"), g[:, s % 2, :],
                                   cb[:, e0 * P:(e0 + 2) * P], ALU.mult).then_inc(S["gated_ready"], 1)

            def body(r):
                i, low = r
                mid, tail = has_pair(low - 1), has_pair(low - 2)
                for j in range(4):
                    here = has_half(4 * low + j)
                    if j == 0 and low == -1:
                        normalize(r, 1, 1, xin, ve1, nm1, rs1, xn, "v_done")
                        constants()
                    if j == 0 and tail:
                        weigh(r, -2, 1)
                    if j == 1 and tail:
                        weigh(r, -2, 3)
                    if here:
                        band_cut(r, j, 0)
                    if j == 0 and has_pair(low + 1):
                        wait(pool, "parts_out", r, lambda i: 16 * 4 * (i + 1))
                        wait(pool, "part2_ready", r, lambda i: i + 2)
                        pool.tensor_tensor(parts[:, :, 2, :], rest[:, :, :], parts[:, :, 1, :],
                                           ALU.subtract).then_inc(S["parts_ready"], 1)
                    if j == 0 and tail:
                        weigh(r, -2, 2)
                    if j == 1 and mid:
                        normalize(r, -1, 2, x2, ve2, nm2, rs2, xn2, "xt_done")
                    if j == 1 and tail:
                        weigh(r, -2, 4)
                    if j == 3 and has_pair(low + 2):
                        normalize(r, 2, 1, xin, ve1, nm1, rs1, xn, "v_done")
                    if here:
                        band_cut(r, j, 1)
                    if j == 3 and mid:
                        spread(r, -1)

            run(pool, body)

        @block.vector
        def _(dve):
            link = Link(dve, S["dve_link"])
            dve.memset(wqk[:, :, :], 0.0).then_inc(S["zeros_ready"], 1)
            dve.memset(wv[:, :], 0.0).then_inc(S["zeros_ready"], 1)
            dve.memset(wo[:, :, :], 0.0).then_inc(S["zeros_ready"], 1)
            dve.memset(wct[:, :], 0.0).then_inc(S["zeros_ready"], 1)
            dve.memset(zrows[:, :].bitcast(U32), 0).then_inc(S["zeros_ready"], 1)

            def norm_stats(src, stat, mv, ve, nm, ready):
                link(dve.bn_stats(stat[:, :], src[:, :]))
                link.wait(wait_ge=hold)
                link(dve.bn_aggr(mv[:, :], stat[:, :]))
                link.wait()
                dve.tensor_scalar(nm[:, :], mv[:, 0:1], -1.0, None, ALU.mult)
                dve.tensor_scalar(ve[:, :], mv[:, 1:2], EPS, None, ALU.add).then_inc(S[ready], 1)

            def row_max(r, j, n):
                qt = n // 2
                wait(dve, "s_done", r, lambda i: 4 * (4 * i + j + 2) + n + 1, alone=True)
                for hd in range(2):
                    col = 2 * (2 * (n % 2) + hd) + qt
                    ins = dve.tensor_tensor_reduce(masked[:, 2 * n + hd, :], s_ps[:, n % 2, W * hd:W * hd + W], band[:, qt, :], 1.0, NEG,
                                                   ALU.add, ALU.max, mx[:, j % 2, col:col + 1])
                ins.then_inc(S["max_done"], 1)

            def max_head(r, j):
                wait(dve, "mt_done", r, lambda i: 4 * i + j + 1)
                wait(dve, "max_done", r, lambda i: 4 * (4 * i + j + 3))
                dve.tensor_copy(mparts[:, j % 2, 0, :], mx[:, j % 2, :]).then_inc(S["head_ready"], 1)

            def max_part(r, j, step):
                q = j % 2
                if step == 0:
                    wait(dve, "mparts_ready", r, lambda i: 4 * i + j + 2)
                    wait(dve, "head_ready", r, lambda i: 4 * i + j + 3)
                    dve.tensor_tensor(mrest[:, :], mx[:, q, :], mparts[:, q, 0, :], ALU.subtract).then_inc(S["mrest_ready"], 1)
                if step == 1:
                    wait(dve, "mrest_ready", r, lambda i: 4 * i + j + 3)
                    dve.tensor_copy(mparts[:, q, 1, :], mrest[:, :]).then_inc(S["mid_ready"], 1)
                if step == 2:
                    wait(dve, "mid_ready", r, lambda i: 4 * i + j + 3)
                    dve.tensor_tensor(mparts[:, q, 2, :], mrest[:, :], mparts[:, q, 1, :], ALU.subtract).then_inc(S["mparts_ready"], 1)

            def divide_turn(r, b, p):
                wait(dve, "pv_done", r, lambda i: 4 * (i + p) + 2 * b + 2)
                dve.transpose(o1[:, :, :].rearrange("p a b -> p (a b)"), pv_ps[:, :]).then_inc(S["pv_read"], 1)

            def divide_recip(r, b, p):
                wait(dve, "pv_read", r, lambda i: 2 * (i + p) + b + 1)
                link(dve.reciprocal(rden[:, :], o1[:, :, D]))

            def divide(r, b, p):
                link(dve.tensor_tensor(o2[:, :, 0:D], o1[:, :, 0:D], rden[:, :].unsqueeze(2).to_broadcast([P, 16, D]), ALU.mult))

            def divide_back(r, b, p):
                wait(dve, "o_done", r, lambda i: i + p)
                dve.transpose(oT[:, b, :], o2[:, :, :].rearrange("p a b -> p (a b)")).then_inc(S["oT_ready"], 1)

            def hidden(r, o, s):
                n = len(experts_of(s)) * P
                wait(dve, "tanh_done", r, lambda i: SLOTS * (i + o) + s + 1)
                link(dve.scalar_tensor_tensor(out=u[:, 0:n], in0=th[:, 0:n], scalar=1.0, in1=h_ps[:, 0:n],
                                              op0=ALU.add, op1=ALU.mult))
                link.wait()
                if s == 0:
                    wait(dve, "down_done", r, lambda i: SLOTS * (i + o))
                    dst = gwt[:, 0, 0, :]
                else:
                    wait(dve, "gated_ready", r, lambda i: 4 * (i + o) + max(s - 2, 0))
                    dst = g[:, s % 2, 0:n]
                dve.scalar_tensor_tensor(out=dst, in0=u[:, 0:n], scalar=0.5, in1=h_ps[:, 2 * P:2 * P + n],
                                         op0=ALU.mult, op1=ALU.mult).then_inc(S["hidden_ready"], 1)

            def first_rest(r):
                wait(dve, "part1_ready", r, lambda i: 2 * (i + 2))
                wait(dve, "parts_ready", r, lambda i: i + 1)
                for t in range(2):
                    ins = dve.scalar_tensor_tensor(out=rest[:, t, :], in0=m_ps[:, T * t:T * t + T],
                                                   scalar=bqk[:, t:t + 1], in1=parts[:, t, 0, :],
                                                   op0=ALU.add, op1=ALU.subtract)
                ins.then_inc(S["rest_ready"], 1)

            def part_copies(r):
                wait(dve, "part2_ready", r, lambda i: i + 2)
                wait(dve, "parts_out", r, lambda i: 16 * 4 * (i + 1))
                dve.tensor_copy(parts[:, 1, PARTS:TURNS, :], parts[:, 1, 0:TURNS - PARTS, :]).then_inc(S["dup_ready"], 1)

            def next_v(r):
                if r[1] == -1:
                    dve.wait_ge(S["w_v_in"], 16 * 6)
                wait(dve, "v_done", r, lambda i: i + 2)
                wait(dve, "v_ready", r, lambda i: i + 1)
                dve.tensor_tensor(vnext[:, :, :].rearrange("p a d -> p (a d)"), m_ps[:, 0:2 * P],
                                  bv[:, :, :].rearrange("p a d -> p (a d)"), ALU.add).then_inc(S["vnext_ready"], 1)

            def gate(r):
                wait(dve, "ctx_in", r, lambda i: 32 * i)
                wait(dve, "ct_done", r, lambda i: i - 1)
                wait(dve, "o_done", r, lambda i: i)
                dve.scalar_tensor_tensor(out=y[:, :], in0=m_ps[:, 0:T], scalar=0.0, in1=ctx[:, :],
                                         op0=ALU.max, op1=ALU.mult).then_inc(S["y_ready"], 1)

            def residual(r):
                if r[1] == 1:
                    dve.wait_ge(S["w_ct_in"], 16 * 4)
                wait(dve, "x2k_ready", r, lambda i: i - 1)
                wait(dve, "xn2_ready", r, lambda i: i - 1)
                wait(dve, "ct_done", r, lambda i: i)
                dve.scalar_tensor_tensor(out=x2[:, :], in0=m_ps[:, 0:T], scalar=bct[:, 0:1], in1=xres[:, :],
                                         op0=ALU.add, op1=ALU.add).then_inc(S["x2_ready"], 1)
                wait(dve, "x2_ready", r, lambda i: i)
                norm_stats(x2, stat2, mv2, ve2, nm2, "ve2_ready")

            def result(r):
                wait(dve, "x2k_ready", r, lambda i: i - 1)
                wait(dve, "out_done", r, lambda i: 16 * (i - 2))
                wait(dve, "down_done", r, lambda i: SLOTS * (i - 1))
                dve.tensor_tensor(res[:, :], y_ps[:, 0:T], x2k[:, :], ALU.add).then_inc(S["res_ready"], 1)

            def body(r):
                i, low = r
                mid, tail, new = has_pair(low - 1), has_pair(low - 2), has_pair(low + 1)
                for j in range(4):
                    ahead = has_half(4 * low + j + 2)
                    b, p = {0: (1, -1), 3: (0, 0)}.get(j, (0, -99))
                    ends = has_pair(low + p)
                    if ahead:
                        row_max(r, j, 0)
                    if j == 0 and low == -1:
                        dve.wait_ge(S["x_in"], 16)
                        norm_stats(xin, stat1, mv1, ve1, nm1, "ve1_ready")
                        dve.memset(qs[:, :, :, :].rearrange("p a b c -> p (a b c)").bitcast(U32), 0).then_inc(S["zeros_ready"], 1)
                        dve.memset(v[:, :, :, :, :], 1.0).then_inc(S["consts_ready"], 1)
                        dve.memset(o2[:, :, :], 1.0).then_inc(S["consts_ready"], 1)
                        for e in range(NE):
                            dve.memset(iota8[:, e:e + 1], float(e)).then_inc(S["consts_ready"], 1)
                        dve.wait_ge(S["consts_ready"], 2 + NE)
                        dve.wait_ge(S["ident_ready"], 2)
                        dve.wait_ge(S["w_qk_in"], 16 * 8)
                    if j == 0 and ahead:
                        row_max(r, j, 1)
                    if j == 0 and new:
                        first_rest(r)
                    if j == 3 and mid:
                        wait(dve, "gexp_ready", r, lambda i: i)
                        link(dve.reciprocal(grec[:, :], gsum[:, :]))
                        rec_at = link.n
                    if ends:
                        divide_turn(r, b, p)
                    if j == 3 and mid:
                        link.wait(rec_at)
                        link(dve.tensor_scalar(prob[:, :], gexp[:, :], grec[:, 0:1], None, ALU.mult))
                        prob_at = link.n
                    if j != 0 and ahead:
                        row_max(r, j, 1)
                    if j == 3 and mid:
                        link.wait(prob_at, wait_ge=hold)
                        link(dve.max(ptop[:, :], prob[:, :]))
                        top_at = link.n
                    if ends:
                        divide_recip(r, b, p)
                        turned = link.n
                    if j == 1 and mid:
                        gate(r)
                    if j == 2 and tail:
                        result(r)
                    if j == 3 and mid:
                        link.wait(top_at, wait_ge=hold)
                        link(dve.max_index(pidx[:, :], ptop[:, :], prob[:, :]))
                        index_at = link.n
                    if j == 3 and has_pair(low + 2):
                        wait(dve, "x_in", r, lambda i: 16 * (i + 3))
                        norm_stats(xin, stat1, mv1, ve1, nm1, "ve1_ready")
                    if j == 3 and mid:
                        link.wait(index_at)
                        link(dve.tensor_copy(pidf[:, :], pidx[:, 0:2]))
                        float_at = link.n
                        hidden(r, -1, 1)
                        link.wait(float_at)
                        for n in range(2):
                            link(dve.tensor_scalar(pick[:, n, :], iota8[:, :], pidf[:, n:n + 1], ptop[:, n:n + 1],
                                                   ALU.is_equal, ALU.mult))
                        pick_at = link.n
                    if ahead:
                        row_max(r, j, 2)
                    if j == 3 and mid:
                        link.wait(pick_at)
                        wait(dve, "combt_done", r, lambda i: i - 1)
                        dve.tensor_tensor(comb[:, :], pick[:, 0, :], pick[:, 1, :], ALU.add).then_inc(S["comb_ready"], 1)
                    if j == 1 and mid:
                        residual(r)
                    if ahead:
                        row_max(r, j, 3)
                        max_head(r, j)
                    if ends:
                        link.wait(turned)
                        divide(r, b, p)
                        divided = link.n
                    if ahead:
                        max_part(r, j, 0)
                    if ends:
                        link.wait(divided)
                        divide_back(r, b, p)
                    if ahead:
                        max_part(r, j, 1)
                    if j == 0 and new:
                        part_copies(r)
                    if ahead:
                        max_part(r, j, 2)
                    if j == 0 and tail:
                        hidden(r, -2, 3)
                    if j == 0 and new:
                        next_v(r)
                    if j == 1 and tail:
                        hidden(r, -2, 4)
                    if j == 2 and mid:
                        hidden(r, -1, 0)
                        wait(dve, "g_done", r, lambda i: i, alone=True)
                        link(dve.max(gtop[:, :], m_ps[:, 0:NE]))
                        link.wait()
                        dve.tensor_scalar(gdif[:, :], m_ps[:, 0:NE], gtop[:, 0:1], None,
                                          ALU.subtract).then_inc(S["gdif_ready"], 1)
                    if j == 3 and mid:
                        hidden(r, -1, 2)

            run(dve, body, link, DVE_LINKS)

        @block.tensor
        def _(pe):
            def scores(r, j, n):
                slot, qt, g0 = (j + 2) % 4, n // 2, 2 * (n % 2)
                if n == 0:
                    wait(pe, loaded[slot], r, lambda i: 16 * LOADS * (i + (j + 2) // 4 + 1))
                wait(pe, "max_done", r, lambda i: 4 * (4 * i + j + 2) + n - 1)
                for hd in range(2):
                    ins = pe.matmul(s_ps[:, n % 2, W * hd:W * hd + W], qs[:, slot, g0 + hd, P * qt:P * qt + P],
                                    ks[:, slot, g0 + hd, BAND * qt:BAND * qt + W], start=True, stop=True)
                ins.then_inc(S["s_done"], 1)

            def scores_t(r, j, n):
                kt, g0 = n // 2, 2 * (n % 2)
                if n == 0:
                    wait(pe, "row_in", r, lambda i: 16 * (4 * i + j + 1))
                wait(pe, "exp_done", r, lambda i: 4 * (4 * i + j) + n - 1)
                if n == 2 and has_half(4 * r[1] + j + 1):
                    wait(pe, "mt_ready", r, lambda i: 4 * i + j + 2)
                for hd in range(2):
                    ins = pe.matmul(st_ps[:, n % 2, W * hd:W * hd + W], ks[:, j, g0 + hd, P * kt:P * kt + P],
                                    qs[:, j, g0 + hd, BAND * kt:BAND * kt + W], start=True, stop=True)
                ins.then_inc(S["st_done"], 1)

            def turn_max(r, j):
                wait(pe, "exp_done", r, lambda i: 4 * (4 * i + j) - 1)
                wait(pe, "mt_ready", r, lambda i: 4 * i + j + 1)
                wait(pe, "mparts_ready", r, lambda i: 4 * i + j + 2)
                pe.matmul(st_ps[0:PARTS * 2 * HG, 0, 2 * W:], mparts[:, (j + 1) % 2, :, :].rearrange("p a b -> p (a b)"), identb[:, :],
                          start=True, stop=True).then_inc(S["mt_done"], 1)

            def probs_v(r, j, kt):
                slot = (j - 1) % 4
                b, hh = slot // 2, slot % 2
                wait(pe, "band_done", r, lambda i: 4 * (4 * i + j - 1) + 2 * kt + 2)
                if kt == 0:
                    wait(pe, "v_ready", r, lambda i: i + (j + 3) // 4)
                    if hh == 0:
                        wait(pe, "pv_read", r, lambda i: (4 * i + j - 1) // 2 if isinstance(i, int) else 2 * i + (j - 1) // 2)
                for gq in range(HG):
                    ins = pe.matmul(pv_ps[32 * gq:32 * gq + 32, T * hh + BAND * kt:T * hh + BAND * kt + W],
                                    v[:, kt, b, HG * hh + gq, :], pt[:, (j - 1) % 2, kt, gq, :],
                                    start=(kt == 0), stop=(kt == 1), skip_group_check=True)
                if kt == 1:
                    ins.then_inc(S["pv_done"], 1)

            def up(r, o, s):
                es = experts_of(s)
                wait(pe, "hidden_ready", r, lambda i: SLOTS * (i + o) + s)
                if s == 0:
                    wait(pe, "xt_ready", r, lambda i: i + o + 1)
                    if r[1] + o == 0:
                        pe.wait_ge(S["w_ffn_in"], 16 * 6)
                for t, w in enumerate((w1, w3)):
                    for n, e in enumerate(es):
                        c0 = (2 * t + n) * P
                        for c in range(2):
                            ins = pe.matmul(h_ps[:, c0:c0 + P], w[:, c, e * INTER:(e + 1) * INTER], xn2T[:, c, :],
                                            start=(c == 0), stop=(c == 1))
                ins.then_inc(S["up_done"], 1)

            def down(r, o, s):
                es = experts_of(s)
                if s == 0:
                    wait(pe, "hidden_ready", r, lambda i: SLOTS * (i + o) + 1)
                    wait(pe, "res_ready", r, lambda i: i + o)
                else:
                    wait(pe, "gated_ready", r, lambda i: 4 * (i + o) + s)
                for n, e in enumerate(es):
                    ins = pe.matmul(y_ps[:, 0:T], gwt[:, s % 2, n, :], w2[:, e, :],
                                    start=(s == 0), stop=(s == SLOTS - 1 and n == 1))
                ins.then_inc(S["down_done"], 1)

            def qk(r):
                wait(pe, "combt_ready", r, lambda i: i - 1)
                if r[1] == -1:
                    pe.wait_ge(S["w_qk_in"], 16 * 8)
                wait(pe, "xn_ready", r, lambda i: i + 2)
                for t in range(2):
                    ins = pe.matmul(m_ps[:, T * t:T * t + T], wqk[:, t, :], xn[:, :], start=True, stop=True)
                ins.then_inc(S["qk_done"], 1)

            def project_v(r):
                wait(pe, "part1_ready", r, lambda i: 2 * (i + 2))
                wait(pe, "rest_ready", r, lambda i: i + 2)
                if r[1] == -1:
                    pe.wait_ge(S["w_v_in"], 16 * 6)
                for kt in range(2):
                    ins = pe.matmul(m_ps[:, P * kt:P * kt + P], xn[:, P * kt:P * kt + P], wv[:, :], start=True, stop=True)
                ins.then_inc(S["v_done"], 1)

            def project_o(r):
                wait(pe, "vnext_ready", r, lambda i: min(i + 2, PAIRS) if isinstance(i, int) else i + 2)
                if r[1] == 1:
                    pe.wait_ge(S["w_o_in"], 16 * 9)
                wait(pe, "oT_ready", r, lambda i: 2 * i)
                for b in range(2):
                    for hh in range(2):
                        ins = pe.matmul(m_ps[C * b:C * b + C, 0:T], wo[:, hh, :], oT[:, b, T * hh:T * hh + T],
                                        start=(hh == 0), stop=(hh == 1))
                ins.then_inc(S["o_done"], 1)

            def project_ct(r):
                if r[1] == 1:
                    pe.wait_ge(S["w_ct_in"], 16 * 4)
                wait(pe, "y_ready", r, lambda i: i)
                pe.matmul(m_ps[:, 0:T], wct[:, :], y[:, :], start=True, stop=True).then_inc(S["ct_done"], 1)

            def turn_x(r):
                wait(pe, "x2_ready", r, lambda i: i)
                wait(pe, "xn2_ready", r, lambda i: i)
                for c in range(2):
                    ins = pe.transpose(m_ps[:, P * c:P * c + P], xn2[:, P * c:P * c + P], ident[:, :])
                ins.then_inc(S["xt_done"], 1)

            def logits(r):
                if r[1] == 1:
                    pe.wait_ge(S["w_gate_in"], 16)
                wait(pe, "xt_ready", r, lambda i: i)
                for c in range(2):
                    ins = pe.matmul(m_ps[0:NE, 0:P], gw[:, c, :], xn2T[:, c, :], start=(c == 0), stop=(c == 1))
                ins.then_inc(S["gt_done"], 1)

            def turn_logits(r):
                wait(pe, "gt_ready", r, lambda i: i, alone=True)
                pe.transpose(m_ps[:, 0:NE], gT[:, :], ident[0:NE, 0:NE]).then_inc(S["g_done"], 1)

            def turn_comb(r):
                wait(pe, "gdif_ready", r, lambda i: i)
                wait(pe, "comb_ready", r, lambda i: i)
                pe.transpose(m_ps[0:NE, 0:P], comb[:, :], ident[:, :]).then_inc(S["combt_done"], 1)

            def body(r):
                i, low = r
                mid, tail, new = has_pair(low - 1), has_pair(low - 2), has_pair(low + 1)
                for j in range(4):
                    here, ahead, rows, back = (has_half(4 * low + j + d) for d in (0, 2, 1, -1))

                    def s(n):
                        if ahead:
                            scores(r, j, n)

                    def t(n):
                        if here:
                            scores_t(r, j, n)

                    def pv(*kts):
                        if back:
                            for kt in kts:
                                probs_v(r, j, kt)

                    if rows:
                        turn_max(r, j)
                    t(0)
                    s(0)
                    if j == 0:
                        if new:
                            qk(r)
                        s(1)
                        t(1)
                        pv(0, 1)
                        s(2)
                        if tail:
                            up(r, -2, 3)
                        t(2)
                        s(3)
                        t(3)
                        if new:
                            project_v(r)
                        if tail:
                            down(r, -2, 1)
                            down(r, -2, 2)
                    if j == 1:
                        pv(0, 1)
                        s(1)
                        t(1)
                        if mid:
                            project_o(r)
                        if tail:
                            up(r, -2, 4)
                        s(2)
                        t(2)
                        if mid:
                            project_ct(r)
                        s(3)
                        if tail:
                            down(r, -2, 3)
                        t(3)
                    if j == 2:
                        s(1)
                        t(1)
                        if tail:
                            down(r, -2, 4)
                        s(2)
                        if mid:
                            turn_x(r)
                        t(2)
                        s(3)
                        pv(0, 1)
                        if mid:
                            logits(r)
                            up(r, -1, 0)
                        t(3)
                        if mid:
                            turn_logits(r)
                    if j == 3:
                        s(1)
                        t(1)
                        if mid:
                            down(r, -1, 0)
                            up(r, -1, 1)
                        pv(0, 1)
                        s(2)
                        t(2)
                        s(3)
                        if mid:
                            up(r, -1, 2)
                            turn_comb(r)
                        t(3)

            pe.wait_ge(S["ident_ready"], 2)
            run(pe, body)


DVE_LINKS = 21

_IN = ["x", "ctx_in", "w_qkT", "b_qk", "w_vT", "b_v", "w_oT", "b_o", "w_ct", "b_ct", "gate_wT", "w1T", "w3T", "w2T",
       "ws1T", "ws3T", "ws2T"]


def kernel(x, ctx_2048, L0_xattn_w_in, L0_xattn_b_in, L0_xattn_w_out, L0_xattn_b_out, L0_xattn_w_ct, L0_xattn_b_ct,
           L0_ffn_gate_w, L0_ffn_w1, L0_ffn_w2, L0_ffn_w3, L0_ffn_ws1, L0_ffn_ws2, L0_ffn_ws3):
    import numpy as np
    import concourse.bacc as bacc
    from concourse.bass_utils import run_bass_kernel_spmd

    a = {k: np.asarray(t) for k, t in locals().items() if k not in ("np", "bacc", "run_bass_kernel_spmd")}
    w_in, b_in = a["L0_xattn_w_in"], a["L0_xattn_b_in"]
    w_qk = w_in[:2 * C].reshape(2, H, D, C).transpose(3, 0, 2, 1).reshape(C, 2 * C)
    b_qk = b_in[:2 * C].reshape(2, H, D).transpose(0, 2, 1).reshape(2 * C, 1)
    ins = {
        "x": a["x"].reshape(B * C, T), "ctx_in": a["ctx_2048"].reshape(B * C, T),
        "w_qkT": w_qk, "b_qk": b_qk,
        "w_vT": w_in[2 * C:].T, "b_v": b_in[2 * C:].reshape(1, C),
        "w_oT": a["L0_xattn_w_out"].T, "b_o": a["L0_xattn_b_out"].reshape(1, C),
        "w_ct": a["L0_xattn_w_ct"], "b_ct": a["L0_xattn_b_ct"].reshape(C, 1),
        "gate_wT": a["L0_ffn_gate_w"].T,
        "w1T": a["L0_ffn_w1"].transpose(2, 0, 1).reshape(T, NE * INTER),
        "w3T": a["L0_ffn_w3"].transpose(2, 0, 1).reshape(T, NE * INTER),
        "w2T": a["L0_ffn_w2"].transpose(2, 0, 1),
        "ws1T": a["L0_ffn_ws1"].T, "ws3T": a["L0_ffn_ws3"].T, "ws2T": a["L0_ffn_ws2"].T,
    }
    nc = bacc.Bacc("TRN2", target_bir_lowering=False, num_devices=1)
    arrays, args = {}, []
    for name in _IN:
        t = np.ascontiguousarray(ins[name])
        arrays[f"in_{name}"] = t
        args.append(nc.dram_tensor(f"in_{name}", t.shape, mybir.dt.from_np(t.dtype), kind="ExternalInput").ap())
    args.append(nc.dram_tensor("out_0", (B * C, T), F32, kind="ExternalOutput").ap())
    build(nc, *args)
    r = run_bass_kernel_spmd(nc, [arrays], core_ids=[0])
    return r.results[0]["out_0"].reshape(B, C, T)
```

```python
from contextlib import ExitStack

import concourse.bass as bass
from concourse import mybir

F32 = mybir.dt.float32
BF16 = mybir.dt.bfloat16
U32 = mybir.dt.uint32
ALU = mybir.AluOpType
ACT = mybir.ActivationFunctionType

P = 128
B, C, T = 16, 64, 256
PAIRS = B * C // P
HALVES = 4 * PAIRS
H, D = 8, 8
HG = 4
BAND = 64
W = P + BAND
NE, INTER = 8, 128
PARTS = 3
SPAN = PARTS * D
MROW = 96
EPS = 1e-5
NEG = -3.0e38
SLOTS = 5
LOADS = 3
TURNS = 2 * PARTS - 1
LOOP_LO, LOOP_HI = 2, PAIRS - 2


def experts_of(s):
    return [NE] if s == 0 else [2 * s - 2, 2 * s - 1]


class Link:

    def __init__(self, eng, sem):
        self.eng, self.sem, self.base, self.n = eng, sem, 0, 0

    def __call__(self, ins):
        self.n += 1
        ins.then_inc(self.sem, 1)
        return self.n

    def at(self, n=None):
        return self.base + (n or self.n)

    def enter(self, i, per):
        self.start, self.per = self.base + self.n, per
        self.base, self.n = (i - LOOP_LO) * per + self.start, 0

    def leave(self):
        assert self.n == self.per, f"{self.n} links in an iteration"
        self.base, self.n = self.start + (LOOP_HI - LOOP_LO) * self.per, 0


def build(nc, x, ctx_in, w_qk, b_qk, w_v, b_v, w_o, w_ct, b_ct, w_gate, w_1, w_3, w_2, out):
    with ExitStack() as st:
        def sb(name, shape, dt=F32):
            return st.enter_context(nc.sbuf_tensor(name, shape, dt))

        def ps(name, shape):
            return st.enter_context(nc.psum_tensor(name, shape, F32))

        def sem(name):
            return st.enter_context(nc.semaphore(name))

        s_ps = ps("s_ps", [P, 2, 512])
        st_ps = ps("st_ps", [P, 2, 512])
        h_ps = ps("h_ps", [P, 512])
        y_ps = ps("y_ps", [P, 512])
        pv_ps = ps("pv_ps", [P, 512])
        m_ps = ps("m_ps", [P, 512])

        q_dram = nc.dram_tensor("q_parts", (2 * PAIRS, PARTS, D * H, T), BF16, kind="Internal").ap()
        k_dram = nc.dram_tensor("k_parts", (2 * PAIRS, TURNS, D * H, T), BF16, kind="Internal").ap()

        wqk = sb("wqk", [P, 2, P])
        bqk = sb("bqk", [P, 2])
        wv = sb("wv", [P, P])
        bv = sb("bv", [P, 2, P])
        wo = sb("wo", [P, 2, C])
        wct = sb("wct", [P, P])
        bct = sb("bct", [P, 1])
        gw = sb("gw", [P, 2, NE])
        w1 = sb("w1", [P, 2, (NE + 1) * INTER])
        w3 = sb("w3", [P, 2, (NE + 1) * INTER])
        w2 = sb("w2", [P, NE + 1, T])
        ident = sb("ident", [P, P])
        identb = sb("identb", [P, P], BF16)
        band = sb("band", [P, 2, W])
        iota8 = sb("iota8", [P, NE])
        mhalf = sb("mhalf", [P, 1])
        zrows = sb("zrows", [PARTS, HG * T], BF16)

        xin = sb("xin", [P, T])
        xn = sb("xn", [P, T])
        stat1, mv1, ve1, nm1, rs1 = sb("stat1", [P, 6]), sb("mv1", [P, 2]), sb("ve1", [P, 1]), sb("nm1", [P, 1]), sb("rs1", [P, 1])
        parts = sb("parts", [P, 2, TURNS, T], BF16)
        rest = sb("rest", [P, 2, T])
        qs = sb("qs", [P, 4, HG, T], BF16)
        ks = sb("ks", [P, 4, HG, T], BF16)
        masked = sb("masked", [P, 8, W])
        mx = sb("mx", [P, 2, 2 * HG])
        mparts = sb("mparts", [P, 2, PARTS, 2 * HG], BF16)
        mrest = sb("mrest", [P, 2 * HG])
        mt = sb("mt", [PARTS * 2 * HG, 2, P], BF16)
        pt = sb("pt", [P, 2, 2, HG, W])
        v = sb("v", [P, 2, 2, H, 32])
        vnext = sb("vnext", [P, 2, P])
        o1 = sb("o1", [P, 16, 32])
        rden = sb("rden", [P, 16])
        o2 = sb("o2", [P, 16, 32])
        oT = sb("oT", [P, 2, 2 * T])

        ctx = sb("ctx", [P, T])
        xres = sb("xres", [P, T])
        y = sb("y", [P, T])
        x2 = sb("x2", [P, T])
        x2k = sb("x2k", [P, T])
        stat2, mv2, ve2, nm2, rs2 = sb("stat2", [P, 6]), sb("mv2", [P, 2]), sb("ve2", [P, 1]), sb("nm2", [P, 1]), sb("rs2", [P, 1])
        xn2 = sb("xn2", [P, T])
        xn2T = sb("xn2T", [P, 2, P])
        gT = sb("gT", [NE, P])
        gtop, gdif, gexp, gsum, grec = (sb("gtop", [P, 8]), sb("gdif", [P, NE]), sb("gexp", [P, NE]),
                                        sb("gsum", [P, 1]), sb("grec", [P, 1]))
        prob, ptop, pidx, pidf = sb("prob", [P, NE]), sb("ptop", [P, 8]), sb("pidx", [P, 8], U32), sb("pidf", [P, 2])
        pick, comb, combT, crow, cb = (sb("pick", [P, 2, NE]), sb("comb", [P, NE]), sb("combT", [NE, P]),
                                       sb("crow", [1, NE * P]), sb("cb", [P, NE * P]))
        th = sb("th", [P, 2 * P])
        u = sb("u", [P, 2, 2 * P])
        h3 = sb("h3", [P, 2, 2 * P])
        g = sb("g", [P, 2, 2 * P])
        gwt = sb("gwt", [P, 2, 2, P])
        res = sb("res", [P, T])

        NAMES = """x_in ctx_in w_qk_in w_v_in w_o_in w_ct_in w_gate_in w_ffn_in parts_out row_in crow_in out_done
            consts_ready head_ready mrest_ready mid_ready dup_ready x2k_ready zeros_ready ident_ready ks_ready
            ve1_ready rs1_ready xn_ready v_done vnext_ready v_ready qk_done part1_ready rest_ready part2_ready parts_ready
            s_done max_done mparts_ready mt_done mt_ready st_done exp_done band_done pv_done pv_read
            oT_ready o_done y_ready ct_done x2_ready ve2_ready rs2_ready xn2_ready xt_done xt_ready
            gt_done gt_ready g_done gdif_ready gexp_ready comb_ready combt_done combt_ready cb_ready
            up_done tanh_done silu_ready branch_ready hidden_ready gated_ready down_done res_ready
            dve_link pool_link held_sync held_pool held_vector held_tensor""".split()
        S = {n: sem(n) for n in NAMES}
        loaded = [sem(f"loaded{j}") for j in range(4)]


        def at(r, value):
            i, low = r
            return value(i) if value(low) > 0 else 0

        def parts_step(j, r):
            i, low = r
            if j == 3 and low >= 0 and has_pair(low + 2):
                return (i + 1, low + 1)
            return {0: (-1, -1), 1: (0, 0)}.get(j) if low == -1 else None

        def run(eng, body, link=None, per=0):
            for i in range(-1, LOOP_LO):
                body((i, i))
            with eng.Fori(LOOP_LO, LOOP_HI) as i:
                if link:
                    link.enter(i, per)
                body((i, LOOP_LO))
                if link:
                    link.leave()
            for i in range(LOOP_HI, PAIRS + 2):
                body((i, i))

        def has_half(k):
            return 0 <= k < HALVES

        def has_pair(p):
            return 0 <= p < PAIRS

        def h_bank(r, o, s):
            return s_ps[:, 0, :] if r[1] + o == PAIRS - 1 and s % 2 else h_ps[:, :]

        def buffer_free(o, s):
            return lambda i: SLOTS * (i + o) + {0: 0, 1: -1}.get(s, s - 1)

        def hidden(eng, r, o, s):
            n = len(experts_of(s)) * P
            eng.wait_ge(S["silu_ready"], at(r, lambda i: SLOTS * (i + o) + s + 1))
            eng.wait_ge(S["branch_ready"], at(r, lambda i: SLOTS * (i + o) + s + 1))
            if s == 0:
                eng.wait_ge(S["down_done"], at(r, lambda i: SLOTS * (i + o)))
                dst = gwt[:, 0, 0, :]
            else:
                eng.wait_ge(S["gated_ready"], at(r, lambda i: 4 * (i + o) + max(s - 2, 0)))
                dst = g[:, s % 2, :]
            eng.tensor_tensor(dst, u[:, s % 2, 0:n], h3[:, s % 2, 0:n], ALU.mult).then_inc(S["hidden_ready"], 1)

        block = st.enter_context(nc.Block())

        @block.sync
        def _(sp):
            sp.dma_start(xin[:, :], x[0:P, :]).then_inc(S["x_in"], 16)
            sp.dma_start(wqk[:, :, :], w_qk).then_inc(S["w_qk_in"], 16)
            sp.dma_start(bqk[:, :], b_qk).then_inc(S["w_qk_in"], 16)
            sp.dma_start(wv[:, :], w_v).then_inc(S["w_v_in"], 16)
            sp.dma_start(bv[:, :, :], b_v.to_broadcast([P, 2 * P])).then_inc(S["w_v_in"], 16)
            sp.dma_start(w1[:, :, :], w_1.rearrange("(c p) e -> p c e", p=P)).then_inc(S["w_ffn_in"], 16)

            sp.dma_start(wo[:, :, :], w_o).then_inc(S["w_o_in"], 16)
            sp.dma_start(wct[:, :], w_ct).then_inc(S["w_ct_in"], 16)
            sp.dma_start(bct[:, :], b_ct).then_inc(S["w_ct_in"], 16)
            sp.dma_start(gw[:, :, :], w_gate.rearrange("(c p) e -> p c e", p=P)).then_inc(S["w_gate_in"], 16)
            sp.dma_start(w3[:, :, :], w_3.rearrange("(c p) e -> p c e", p=P)).then_inc(S["w_ffn_in"], 16)

            def stacks(i, low, off):
                slot = off % 4
                b, hh = slot // 2, slot % 2
                pair = (i + off // 4, low + off // 4)
                sp.wait_ge(S["st_done"], at((i, low), lambda i: 4 * (4 * i + off - 4 + 1))).then_inc(S["held_sync"], 1)
                sp.wait_ge(S["parts_out"], at(pair, lambda p: 16 * 4 * (p + 1))).then_inc(S["held_sync"], 1)
                if pair[1] == 0:
                    sp.wait_ge(S["zeros_ready"], 2 + slot // 2)
                    sp.wait_ge(S["ks_ready"], 1 + slot // 2)
                for dst, src, turn in ((qs, q_dram, 0), (ks, k_dram, D)):
                    v0 = src[bass.ds(2 * pair[0] + b, 1)].rearrange("o a (d h) t -> (o a d) (h t)", h=H)[0:SPAN, HG * hh * T:HG * (hh + 1) * T]
                    three = bass.AP(tensor=v0.tensor, offset=v0.offset, ap=[[turn * H * T, PARTS], [H * T, SPAN], [1, HG * T]])
                    sp.dma_start(dst[0:PARTS * SPAN, slot, :, :].rearrange("r h t -> r (h t)"), three).then_inc(loaded[slot], 16)
                sp.dma_start(qs[MROW:MROW + PARTS, slot, :, :], zrows[:, :].rearrange("a (h t) -> a h t", h=HG)).then_inc(loaded[slot], 16)

            def parts_go(i):
                sp.wait_ge(S["parts_ready"], i + 2).then_inc(S["held_sync"], 1)
                sp.wait_ge(S["dup_ready"], i + 2).then_inc(S["held_sync"], 1)
                for b in range(2):
                    for t, (dram, n) in enumerate(((q_dram, PARTS), (k_dram, TURNS))):
                        sp.dma_start(dram[bass.ds(2 * (i + 1) + b, 1)].rearrange("o a r t -> (o r) a t"),
                                     parts[C * b:C * b + C, t, 0:n, :]).then_inc(S["parts_out"], 16)

            def body(r):
                i, low = r
                for j in range(4):
                    klow = 4 * low + j
                    if j == 0 and low == -1:
                        sp.wait_ge(S["xn_ready"], 1)
                        sp.dma_start(xin[:, :], x[P:2 * P, :]).then_inc(S["x_in"], 16)
                    if j == 1 and has_pair(low + 1):
                        stacks(i, low, 4)
                    if has_half(klow + 1):
                        off = j + 1
                        slot, par = off % 4, off % 2
                        sp.wait_ge(S["mt_ready"], at(r, lambda i: 4 * i + off + 1)).then_inc(S["held_sync"], 1)
                        dst = qs[MROW:MROW + PARTS, slot, :, :].rearrange("a h (q t) -> a (h q) t", q=2)
                        sp.dma_start(dst, mt[:, par, :]).then_inc(S["row_in"], 16)
                    if j > 0 and has_pair(low + 1):
                        stacks(i, low, j + 4)
                    if j < 3 and low == 0:
                        third = slice(3 * j, 3 * j + 3)
                        sp.dma_start(w2[:, third, :], w_2[:, third, :]).then_inc(S["w_ffn_in"], 16)
                    if j == 2 and has_pair(low):
                        sp.wait_ge(S["x2_ready"], at(r, lambda i: i)).then_inc(S["held_sync"], 1)
                        sp.dma_start(ctx[:, :], ctx_in[bass.ds(i * P, P), :]).then_inc(S["ctx_in"], 16)
                        sp.dma_start(xres[:, :], x[bass.ds(i * P, P), :]).then_inc(S["ctx_in"], 16)
                    if j == 0 and has_pair(low + 1) and low != 0:
                        parts_go(i)
                    if j == 3 and low == -1:
                        parts_go(0)
                    if j == 0 and has_pair(low + 2) and low != -1:
                        sp.wait_ge(S["xn_ready"], at(r, lambda i: i + 2)).then_inc(S["held_sync"], 1)
                        sp.dma_start(xin[:, :], x[bass.ds((i + 2) * P, P), :]).then_inc(S["x_in"], 16)
                    if j == 2 and has_pair(low - 2):
                        sp.wait_ge(S["res_ready"], at(r, lambda i: i - 1)).then_inc(S["held_sync"], 1)
                        sp.dma_start(out[bass.ds((i - 2) * P, P), :], res[:, :]).then_inc(S["out_done"], 16)
                    if j == 3 and has_pair(low - 1):
                        sp.wait_ge(S["combt_ready"], at(r, lambda i: i)).then_inc(S["held_sync"], 1)
                        sp.wait_ge(S["cb_ready"], at(r, lambda i: i - 1)).then_inc(S["held_sync"], 1)
                        sp.dma_start(crow[:, :].rearrange("a (e t) -> a e t", e=NE), combT[:, :]).then_inc(S["crow_in"], 16)

            run(sp, body)
            sp.wait_ge(S["out_done"], 16 * (PAIRS + 1))

        @block.scalar
        def _(act):
            def exp(r, j, n):
                i, low = r
                kt, g0 = n // 2, 2 * (n % 2)
                act.wait_ge(S["st_done"], at(r, lambda i: 4 * (4 * i + j) + n + 1))
                if n == 0:
                    act.wait_ge(S["pv_done"], at(r, lambda i: 4 * i + j - 1))
                act.activation(pt[:, j % 2, kt, g0:g0 + 2, :], st_ps[:, n % 2, 0:2 * W].rearrange("p (h w) -> p h w", h=2),
                               ACT.Exp, scale=float(D) ** -0.5).then_inc(S["exp_done"], 1)

            def max_rows(r, j):
                act.wait_ge(S["mt_done"], at(r, lambda i: 4 * i + j + 2))
                if has_half(4 * r[1] + j):
                    act.wait_ge(S["st_done"], at(r, lambda i: 4 * (4 * i + j) + 2))
                act.wait_ge(S["row_in"], at(r, lambda i: 16 * (4 * i + j)))
                act.copy(mt[:, (j + 1) % 2, :], st_ps[0:PARTS * 2 * HG, 1, 2 * W:]).then_inc(S["mt_ready"], 1)

            def tanh(r, o, s):
                n = len(experts_of(s)) * P
                act.wait_ge(S["up_done"], at(r, lambda i: SLOTS * (i + o) + s + 1))
                act.wait_ge(S["silu_ready"], at(r, lambda i: SLOTS * (i + o) + s))
                h = h_bank(r, o, s)
                act.activation(th[:, 0:n], h[:, 0:n], ACT.Tanh, scale=0.5).then_inc(S["tanh_done"], 1)
                act.wait_ge(S["hidden_ready"], at(r, buffer_free(o, s)))
                act.activation(h3[:, s % 2, 0:n], h[:, 2 * P:2 * P + n], ACT.Identity, scale=0.5).then_inc(S["branch_ready"], 1)

            def body(r):
                i, low = r
                mid, tail = has_pair(low - 1), has_pair(low - 2)
                for j in range(4):
                    here = has_half(4 * low + j)
                    if here:
                        exp(r, j, 0)
                    made = parts_step(j, r)
                    if made:
                        act.wait_ge(S["qk_done"], at(made, lambda i: i + 2))
                        act.wait_ge(S["parts_out"], at(made, lambda i: 16 * 4 * (i + 1)))
                        for t in range(2):
                            act.activation(parts[:, t, 0, :], m_ps[:, T * t:T * t + T], ACT.Identity,
                                           bias=bqk[:, t:t + 1]).then_inc(S["part1_ready"], 1)
                    if has_half(4 * low + j + 1):
                        max_rows(r, j)
                    if here:
                        exp(r, j, 1)
                    if j == 3 and mid:
                        tanh(r, -1, 1)
                    if made:
                        act.wait_ge(S["rest_ready"], at(made, lambda i: i + 2))
                        act.copy(parts[:, :, 1, :], rest[:, :, :]).then_inc(S["part2_ready"], 1)
                        act.wait_ge(S["part2_ready"], at(made, lambda i: i + 2))
                        act.copy(parts[:, 1, PARTS:TURNS, :], parts[:, 1, 0:TURNS - PARTS, :]).then_inc(S["dup_ready"], 1)
                    if j == 0 and has_pair(low):
                        act.wait_ge(S["vnext_ready"], at(r, lambda i: i + 1))
                        act.wait_ge(S["pv_done"], at(r, lambda i: 4 * i))
                        act.copy(v[:, :, :, :, 0:D].rearrange("p a b h d -> p (a b h) d"),
                                 vnext[:, :, :].rearrange("p a (h d) -> p (a h) d", d=D)).then_inc(S["v_ready"], 1)
                    if j == 2 and mid:
                        act.wait_ge(S["xt_done"], at(r, lambda i: i))
                        act.wait_ge(S["up_done"], at(r, lambda i: SLOTS * (i - 1)))
                        act.copy(xn2T[:, :, :].rearrange("p c t -> p (c t)"), m_ps[:, 0:2 * P]).then_inc(S["xt_ready"], 1)
                    if here:
                        exp(r, j, 2)
                    if j == 2 and mid:
                        act.wait_ge(S["gt_done"], at(r, lambda i: i))
                        act.copy(gT[:, :], m_ps[0:NE, 0:P]).then_inc(S["gt_ready"], 1)
                    if here:
                        exp(r, j, 3)
                    if j == 0 and tail:
                        tanh(r, -2, 3)
                    if j == 1 and tail:
                        tanh(r, -2, 4)
                    if j == 2 and mid:
                        tanh(r, -1, 0)
                    if j == 3 and mid and low != PAIRS:
                        tanh(r, -1, 2)
                    if j == 3 and mid:
                        act.wait_ge(S["combt_done"], at(r, lambda i: i))
                        act.wait_ge(S["crow_in"], at(r, lambda i: 16 * (i - 1)))
                        act.copy(combT[:, :], m_ps[0:NE, 0:P]).then_inc(S["combt_ready"], 1)
                    if j == 3 and low == PAIRS:
                        tanh(r, -1, 2)
                    if j == 2 and mid:
                        act.wait_ge(S["gdif_ready"], at(r, lambda i: i))
                        act.activation(gexp[:, :], gdif[:, :], ACT.Exp, accum_out=gsum[:, :]).then_inc(S["gexp_ready"], 1)
                        act.wait_ge(S["x2_ready"], at(r, lambda i: i))
                        act.wait_ge(S["res_ready"], at(r, lambda i: i - 1))
                        act.copy(x2k[:, :], x2[:, :]).then_inc(S["x2k_ready"], 1)

            run(act, body)

        @block.gpsimd
        def _(pool):
            link = Link(pool, S["pool_link"])
            link(pool.memset(mhalf[:, :], -0.5))
            pool.wait_ge(S["pool_link"], link.at())

            def zero_keys(half):
                two = slice(2 * half, 2 * half + 2)
                link(pool.memset(ks[:, two, :, :].rearrange("p a b c -> p (a b c)").bitcast(U32), 0))
                return lambda: pool.memset(ks[MROW:MROW + PARTS, two, :, :], -1.0).then_inc(S["ks_ready"], 1)

            def constants():
                link(pool.memset(ident[:, :], 0.0))
                link(pool.memset(identb[:, :], 0.0))
                link(pool.memset(band[:, :, :], 0.0))
                pool.wait_ge(S["pool_link"], link.at())
                for sign in (1, -1):
                    for t in range(2):
                        link(pool.affine_select(out=band[:, t, :], in_=band[:, t, :], compare_op=ALU.is_ge, fill=NEG,
                                                base=BAND + sign * (BAND - P) * t, pattern=[[sign, W]],
                                                channel_multiplier=-sign))
                    pool.wait_ge(S["pool_link"], link.at())
                for t in (ident, identb):
                    pool.affine_select(out=t[:, :], in_=t[:, :], compare_op=ALU.not_equal, fill=1.0, base=0,
                                       pattern=[[-1, P]], channel_multiplier=1).then_inc(S["ident_ready"], 1)

            def normalize(r, p, n, src, ve, nm, rs, dst, used):
                pool.wait_ge(S[f"ve{n}_ready"], at(r, lambda i: i + p + 1))
                pool.tensor_tensor(rs[:, :], ve[:, :], mhalf[:, :], ALU.pow).then_inc(S[f"rs{n}_ready"], 1)
                pool.wait_ge(S[used], at(r, lambda i: i + p))
                pool.wait_ge(S[f"rs{n}_ready"], at(r, lambda i: i + p + 1)).then_inc(S["held_pool"], 1)
                pool.tensor_scalar(dst[:, :], src[:, :], nm[:, 0:1], rs[:, 0:1], ALU.add,
                                   ALU.mult).then_inc(S["xn_ready" if n == 1 else "xn2_ready"], 1)

            def band_cut(r, j, kt):
                pool.wait_ge(S["exp_done"], at(r, lambda i: 4 * (4 * i + j) + 2 * kt + 2)).then_inc(S["held_pool"], 1)
                edge = BAND * (1 + kt)
                low_side = pt[:, j % 2, kt, :, 0:edge]
                high_side = pt[:, j % 2, kt, :, edge:W]
                pool.affine_select(out=low_side, in_=low_side, compare_op=ALU.is_ge, fill=0.0,
                                   base=BAND - BAND * kt, pattern=[[0, HG], [1, edge]],
                                   channel_multiplier=-1).then_inc(S["band_done"], 1)
                pool.affine_select(out=high_side, in_=high_side, compare_op=ALU.is_ge, fill=0.0,
                                   base=BAND + BAND * kt - edge, pattern=[[0, HG], [-1, W - edge]],
                                   channel_multiplier=1).then_inc(S["band_done"], 1)

            def third_parts(r):
                pool.wait_ge(S["parts_out"], at(r, lambda i: 16 * 4 * (i + 1)))
                pool.wait_ge(S["part2_ready"], at(r, lambda i: i + 2))
                pool.tensor_tensor(parts[:, :, 2, :], rest[:, :, :], parts[:, :, 1, :],
                                   ALU.subtract).then_inc(S["parts_ready"], 1)

            def spread(r, o):
                pool.wait_ge(S["gated_ready"], at(r, lambda i: 4 * (i + o)))
                pool.wait_ge(S["crow_in"], at(r, lambda i: 16 * (i + o + 1))).then_inc(S["held_pool"], 1)
                pool.partition_broadcast(cb[:, :], crow[:, :], P).then_inc(S["cb_ready"], 1)

            def weigh(r, o, s):
                e0 = experts_of(s)[0]
                if s == 1:
                    pool.wait_ge(S["cb_ready"], at(r, lambda i: i + o + 1))
                pool.wait_ge(S["hidden_ready"], at(r, lambda i: SLOTS * (i + o) + s + 1))
                if s > 1:
                    pool.wait_ge(S["down_done"], at(r, lambda i: SLOTS * (i + o) + s - 1))
                pool.tensor_tensor(gwt[:, s % 2, :, :].rearrange("p e t -> p (e t)"), g[:, s % 2, :],
                                   cb[:, e0 * P:(e0 + 2) * P], ALU.mult).then_inc(S["gated_ready"], 1)

            def body(r):
                i, low = r
                mid, tail = has_pair(low - 1), has_pair(low - 2)
                for j in range(4):
                    here = has_half(4 * low + j)
                    if j == 0 and low == -1:
                        minus = zero_keys(0)
                        normalize(r, 1, 1, xin, ve1, nm1, rs1, xn, "v_done")
                        constants()
                        pool.wait_ge(S["ident_ready"], 2)
                        minus()
                        pool.wait_ge(S["ks_ready"], 1)
                    if j == 0 and tail:
                        weigh(r, -2, 1)
                    made = parts_step(j, r)
                    if j == 1 and made:
                        normalize(r, 2, 1, xin, ve1, nm1, rs1, xn, "v_done")
                    if made and j != 3:
                        third_parts(made)
                    if j == 1 and tail:
                        if low - 2 < PAIRS - 1:
                            hidden(pool, r, -2, 3)
                        weigh(r, -2, 3)
                    if j == 3 and mid and low != PAIRS:
                        hidden(pool, r, -1, 1)
                    if here:
                        band_cut(r, j, 0)
                    if j == 0 and low == -1:
                        minus = zero_keys(1)
                        pool.wait_ge(S["pool_link"], link.at())
                        minus()
                        pool.wait_ge(S["ks_ready"], 2)
                    if j == 0 and tail:
                        weigh(r, -2, 2)
                    if j == 1 and has_pair(low + 2) and low != -1:
                        normalize(r, 2, 1, xin, ve1, nm1, rs1, xn, "v_done")
                    if j == 1 and mid:
                        normalize(r, -1, 2, x2, ve2, nm2, rs2, xn2, "xt_done")
                    if j == 2 and mid and low != PAIRS:
                        hidden(pool, r, -1, 0)
                    if here:
                        band_cut(r, j, 1)
                    if made and j == 3:
                        third_parts(made)
                    if j == 1 and tail:
                        if low - 2 < PAIRS - 1:
                            hidden(pool, r, -2, 4)
                        weigh(r, -2, 4)
                    if j == 3 and mid and low != PAIRS:
                        hidden(pool, r, -1, 2)
                    if j == 3 and mid:
                        spread(r, -1)

            run(pool, body)

        @block.vector
        def _(dve):
            link = Link(dve, S["dve_link"])
            dve.memset(zrows[:, :].bitcast(U32), 0).then_inc(S["zeros_ready"], 1)

            dve.memset(res[:, 0:1], 0.0).then_inc(S["out_done"], 16)

            def zero_queries(half):
                two = slice(2 * half, 2 * half + 2)
                dve.memset(qs[:, two, :, :].rearrange("p a b c -> p (a b c)").bitcast(U32), 0).then_inc(S["zeros_ready"], 1)

            def norm_stats(src, stat, mv, ve, nm, ready):
                link(dve.bn_stats(stat[:, :], src[:, :]))
                dve.wait_ge(S["dve_link"], link.at()).then_inc(S["held_vector"], 1)
                link(dve.bn_aggr(mv[:, :], stat[:, :]))
                dve.wait_ge(S["dve_link"], link.at())
                dve.tensor_scalar(nm[:, :], mv[:, 0:1], -1.0, None, ALU.mult)
                dve.tensor_scalar(ve[:, :], mv[:, 1:2], EPS, None, ALU.add).then_inc(S[ready], 1)

            def row_max(r, j, n):
                qt = n // 2
                dve.wait_ge(S["s_done"], at(r, lambda i: 4 * (4 * i + j + 2) + n + 1)).then_inc(S["held_vector"], 1)
                for hd in range(2):
                    col = 2 * (2 * (n % 2) + hd) + qt
                    ins = dve.tensor_tensor_reduce(masked[:, 2 * n + hd, :], s_ps[:, n % 2, W * hd:W * hd + W], band[:, qt, :], 1.0, NEG,
                                                   ALU.add, ALU.max, mx[:, j % 2, col:col + 1])
                ins.then_inc(S["max_done"], 1)

            def max_head(r, j):
                dve.wait_ge(S["mt_done"], at(r, lambda i: 4 * i + j + 1))
                dve.wait_ge(S["max_done"], at(r, lambda i: 4 * (4 * i + j + 3)))
                dve.tensor_copy(mparts[:, j % 2, 0, :], mx[:, j % 2, :]).then_inc(S["head_ready"], 1)

            def max_part(r, j, step):
                q = j % 2
                if step == 0:
                    dve.wait_ge(S["mparts_ready"], at(r, lambda i: 4 * i + j + 2))
                    dve.wait_ge(S["head_ready"], at(r, lambda i: 4 * i + j + 3))
                    dve.tensor_tensor(mrest[:, :], mx[:, q, :], mparts[:, q, 0, :], ALU.subtract).then_inc(S["mrest_ready"], 1)
                if step == 1:
                    dve.wait_ge(S["mrest_ready"], at(r, lambda i: 4 * i + j + 3))
                    dve.tensor_copy(mparts[:, q, 1, :], mrest[:, :]).then_inc(S["mid_ready"], 1)
                if step == 2:
                    dve.wait_ge(S["mid_ready"], at(r, lambda i: 4 * i + j + 3))
                    dve.tensor_tensor(mparts[:, q, 2, :], mrest[:, :], mparts[:, q, 1, :], ALU.subtract).then_inc(S["mparts_ready"], 1)

            def divide_turn(r, b, p):
                dve.wait_ge(S["pv_done"], at(r, lambda i: 4 * (i + p) + 2 * b + 2))
                dve.transpose(o1[:, :, :].rearrange("p a b -> p (a b)"), pv_ps[:, :]).then_inc(S["pv_read"], 1)

            def divide_recip(r, b, p):
                dve.wait_ge(S["pv_read"], at(r, lambda i: 2 * (i + p) + b + 1))
                link(dve.reciprocal(rden[:, :], o1[:, :, D]))

            def divide(r, b, p):
                link(dve.tensor_tensor(o2[:, :, 0:D], o1[:, :, 0:D], rden[:, :].unsqueeze(2).to_broadcast([P, 16, D]), ALU.mult))

            def divide_back(r, b, p):
                dve.wait_ge(S["o_done"], at(r, lambda i: i + p))
                dve.transpose(oT[:, b, :], o2[:, :, :].rearrange("p a b -> p (a b)")).then_inc(S["oT_ready"], 1)

            def silu(r, o, s):
                n = len(experts_of(s)) * P
                dve.wait_ge(S["branch_ready"], at(r, lambda i: SLOTS * (i + o) + s + 1))
                dve.wait_ge(S["hidden_ready"], at(r, buffer_free(o, s)))
                dve.scalar_tensor_tensor(out=u[:, s % 2, 0:n], in0=th[:, 0:n], scalar=1.0, in1=h_bank(r, o, s)[:, 0:n],
                                         op0=ALU.add, op1=ALU.mult).then_inc(S["silu_ready"], 1)
                if r[1] + o == PAIRS - 1:
                    hidden(dve, r, o, s)

            def first_rest(r):
                dve.wait_ge(S["part1_ready"], at(r, lambda i: 2 * (i + 2)))
                dve.wait_ge(S["parts_ready"], at(r, lambda i: i + 1))
                for t in range(2):
                    ins = dve.scalar_tensor_tensor(out=rest[:, t, :], in0=m_ps[:, T * t:T * t + T],
                                                   scalar=bqk[:, t:t + 1], in1=parts[:, t, 0, :],
                                                   op0=ALU.add, op1=ALU.subtract)
                ins.then_inc(S["rest_ready"], 1)

            def next_v(r):
                if r[1] == -1:
                    dve.wait_ge(S["w_v_in"], 32)
                dve.wait_ge(S["v_done"], at(r, lambda i: i + 2))
                dve.wait_ge(S["v_ready"], at(r, lambda i: i + 1))
                dve.tensor_tensor(vnext[:, :, :].rearrange("p a d -> p (a d)"), m_ps[:, 0:2 * P],
                                  bv[:, :, :].rearrange("p a d -> p (a d)"), ALU.add).then_inc(S["vnext_ready"], 1)

            def gate(r):
                dve.wait_ge(S["ctx_in"], at(r, lambda i: 32 * i))
                dve.wait_ge(S["ct_done"], at(r, lambda i: i - 1))
                dve.wait_ge(S["o_done"], at(r, lambda i: i))
                dve.scalar_tensor_tensor(out=y[:, :], in0=m_ps[:, 0:T], scalar=0.0, in1=ctx[:, :],
                                         op0=ALU.max, op1=ALU.mult).then_inc(S["y_ready"], 1)

            def residual(r):
                if r[1] == 1:
                    dve.wait_ge(S["w_ct_in"], 32)
                dve.wait_ge(S["x2k_ready"], at(r, lambda i: i - 1))
                dve.wait_ge(S["xn2_ready"], at(r, lambda i: i - 1))
                dve.wait_ge(S["ct_done"], at(r, lambda i: i))
                dve.scalar_tensor_tensor(out=x2[:, :], in0=m_ps[:, 0:T], scalar=bct[:, 0:1], in1=xres[:, :],
                                         op0=ALU.add, op1=ALU.add).then_inc(S["x2_ready"], 1)
                dve.wait_ge(S["x2_ready"], at(r, lambda i: i))
                norm_stats(x2, stat2, mv2, ve2, nm2, "ve2_ready")

            def result(r):
                dve.wait_ge(S["x2k_ready"], at(r, lambda i: i - 1))
                dve.wait_ge(S["out_done"], at(r, lambda i: 16 * (i - 1)))
                dve.wait_ge(S["down_done"], at(r, lambda i: SLOTS * (i - 1)))
                dve.tensor_tensor(res[:, :], y_ps[:, 0:T], x2k[:, :], ALU.add).then_inc(S["res_ready"], 1)

            def body(r):
                i, low = r
                mid, tail, new = has_pair(low - 1), has_pair(low - 2), has_pair(low + 1)
                for j in range(4):
                    ahead = has_half(4 * low + j + 2)
                    b, p = {0: (1, -1), 3: (0, 0)}.get(j, (0, -99))
                    ends = has_pair(low + p)
                    if ahead:
                        row_max(r, j, 0)
                    if j == 0 and tail:
                        silu(r, -2, 2)
                    if j == 0 and low == -1:
                        zero_queries(0)
                        dve.wait_ge(S["x_in"], 16)
                        norm_stats(xin, stat1, mv1, ve1, nm1, "ve1_ready")
                        dve.memset(v[:, :, :, :, :], 1.0).then_inc(S["consts_ready"], 1)
                        dve.memset(o2[:, :, :], 1.0).then_inc(S["consts_ready"], 1)
                        for e in range(NE):
                            dve.memset(iota8[:, e:e + 1], float(e)).then_inc(S["consts_ready"], 1)
                        dve.wait_ge(S["w_qk_in"], 32)
                    if j == 0 and ahead:
                        row_max(r, j, 1)
                    made = parts_step(j, r)
                    if j == 1 and made:
                        dve.wait_ge(S["x_in"], 32)
                        norm_stats(xin, stat1, mv1, ve1, nm1, "ve1_ready")
                    if made and j != 3:
                        first_rest(made)
                    if j == 3 and mid:
                        dve.wait_ge(S["gexp_ready"], at(r, lambda i: i))
                        link(dve.reciprocal(grec[:, :], gsum[:, :]))
                        rec_at = link.n
                    if j == 0 and ends:
                        divide_turn(r, b, p)
                    if j == 3 and mid:
                        dve.wait_ge(S["dve_link"], link.at(rec_at))
                        link(dve.tensor_scalar(prob[:, :], gexp[:, :], grec[:, 0:1], None, ALU.mult))
                        prob_at = link.n
                    if j != 0 and ahead:
                        row_max(r, j, 1)
                    if j == 3 and mid:
                        dve.wait_ge(S["dve_link"], link.at(prob_at)).then_inc(S["held_vector"], 1)
                        link(dve.max(ptop[:, :], prob[:, :]))
                        top_at = link.n
                    if ends:
                        divide_recip(r, b, p)
                        turned = link.n
                    if j == 3 and mid:
                        dve.wait_ge(S["dve_link"], link.at(top_at)).then_inc(S["held_vector"], 1)
                        link(dve.max_index(pidx[:, :], ptop[:, :], prob[:, :]))
                        index_at = link.n
                    if made and j == 3:
                        first_rest(made)
                    if j == 1 and mid:
                        gate(r)
                    if j == 1 and has_pair(low + 2) and low != -1:
                        dve.wait_ge(S["x_in"], at(r, lambda i: 16 * (i + 3)))
                        norm_stats(xin, stat1, mv1, ve1, nm1, "ve1_ready")
                    if ahead:
                        row_max(r, j, 2)
                    if j == 3 and mid and low != PAIRS:
                        silu(r, -1, 1)
                    if j == 3 and mid:
                        dve.wait_ge(S["dve_link"], link.at(index_at))
                        link(dve.tensor_copy(pidf[:, :], pidx[:, 0:2]))
                        float_at = link.n
                    if ends:
                        dve.wait_ge(S["dve_link"], link.at(turned))
                        divide(r, b, p)
                        divided = link.n
                    if j == 3 and mid:
                        dve.wait_ge(S["dve_link"], link.at(float_at))
                        for n in range(2):
                            link(dve.tensor_scalar(pick[:, n, :], iota8[:, :], pidf[:, n:n + 1], ptop[:, n:n + 1],
                                                   ALU.is_equal, ALU.mult))
                        pick_at = link.n
                    if ahead:
                        row_max(r, j, 3)
                    if j == 3 and mid:
                        dve.wait_ge(S["dve_link"], link.at(pick_at))
                        dve.wait_ge(S["combt_done"], at(r, lambda i: i - 1))
                        dve.tensor_tensor(comb[:, :], pick[:, 0, :], pick[:, 1, :], ALU.add).then_inc(S["comb_ready"], 1)
                        if low == PAIRS:
                            silu(r, -1, 1)
                    if j == 1 and mid:
                        residual(r)
                    if ahead:
                        max_head(r, j)
                    if ahead:
                        max_part(r, j, 0)
                    if j == 0 and low == -1:
                        dve.wait_ge(S["consts_ready"], 2 + NE)
                    if j == 0 and new:
                        next_v(r)
                    if ahead:
                        max_part(r, j, 1)
                    if j != 0 and ends:
                        dve.wait_ge(S["dve_link"], link.at(divided))
                        divide_back(r, b, p)
                    if ahead:
                        max_part(r, j, 2)
                    if j == 0 and ends:
                        dve.wait_ge(S["dve_link"], link.at(divided))
                        divide_back(r, b, p)
                    if j == 2 and mid:
                        silu(r, -1, 0)
                    if j == 2 and has_pair(low):
                        divide_turn(r, 0, 0)
                    if j == 0 and tail:
                        silu(r, -2, 3)
                    if j == 0 and low == -1:
                        zero_queries(1)
                        dve.wait_ge(S["ident_ready"], 2)
                    if j == 1 and tail:
                        silu(r, -2, 4)
                    if j == 2 and mid:
                        dve.wait_ge(S["g_done"], at(r, lambda i: i)).then_inc(S["held_vector"], 1)
                        link(dve.max(gtop[:, :], m_ps[:, 0:NE]))
                        dve.wait_ge(S["dve_link"], link.at())
                        dve.tensor_scalar(gdif[:, :], m_ps[:, 0:NE], gtop[:, 0:1], None,
                                          ALU.subtract).then_inc(S["gdif_ready"], 1)
                    if j == 2 and tail:
                        result(r)

            run(dve, body, link, DVE_LINKS)

        @block.tensor
        def _(pe):
            def scores(r, j, n):
                slot, qt, g0 = (j + 2) % 4, n // 2, 2 * (n % 2)
                if n == 0:
                    pe.wait_ge(loaded[slot], at(r, lambda i: 16 * LOADS * (i + (j + 2) // 4 + 1)))
                pe.wait_ge(S["max_done"], at(r, lambda i: 4 * (4 * i + j + 2) + n - 1))
                for hd in range(2):
                    ins = pe.matmul(s_ps[:, n % 2, W * hd:W * hd + W], qs[:, slot, g0 + hd, P * qt:P * qt + P],
                                    ks[:, slot, g0 + hd, BAND * qt:BAND * qt + W], start=True, stop=True)
                ins.then_inc(S["s_done"], 1)

            def scores_t(r, j, n):
                kt, g0 = n // 2, 2 * (n % 2)
                if n == 0:
                    pe.wait_ge(S["row_in"], at(r, lambda i: 16 * (4 * i + j + 1)))
                pe.wait_ge(S["exp_done"], at(r, lambda i: 4 * (4 * i + j) + n - 1))
                if n == 3 and has_half(4 * r[1] + j + 1):
                    pe.wait_ge(S["mt_ready"], at(r, lambda i: 4 * i + j + 2))
                for hd in range(2):
                    ins = pe.matmul(st_ps[:, n % 2, W * hd:W * hd + W], ks[:, j, g0 + hd, P * kt:P * kt + P],
                                    qs[:, j, g0 + hd, BAND * kt:BAND * kt + W], start=True, stop=True)
                ins.then_inc(S["st_done"], 1)

            def turn_max(r, j):
                pe.wait_ge(S["exp_done"], at(r, lambda i: 4 * (4 * i + j)))
                pe.wait_ge(S["mt_ready"], at(r, lambda i: 4 * i + j + 1))
                if r[1] == -1:
                    pe.wait_ge(S["ident_ready"], 2)
                pe.wait_ge(S["mparts_ready"], at(r, lambda i: 4 * i + j + 2))
                pe.matmul(st_ps[0:PARTS * 2 * HG, 1, 2 * W:], mparts[:, (j + 1) % 2, :, :].rearrange("p a b -> p (a b)"), identb[:, :],
                          start=True, stop=True).then_inc(S["mt_done"], 1)

            def probs_v(r, j, kt):
                slot = (j - 1) % 4
                b, hh = slot // 2, slot % 2
                pe.wait_ge(S["band_done"], at(r, lambda i: 4 * (4 * i + j - 1) + 2 * kt + 2))
                if kt == 0:
                    pe.wait_ge(S["v_ready"], at(r, lambda i: i + (j + 3) // 4))
                    if hh == 0:
                        pe.wait_ge(S["pv_read"], at(r, lambda i: (4 * i + j - 1) // 2 if isinstance(i, int) else 2 * i + (j - 1) // 2))
                for gq in range(HG):
                    ins = pe.matmul(pv_ps[32 * gq:32 * gq + 32, T * hh + BAND * kt:T * hh + BAND * kt + W],
                                    v[:, kt, b, HG * hh + gq, :], pt[:, (j - 1) % 2, kt, gq, :],
                                    start=(kt == 0), stop=(kt == 1), skip_group_check=True)
                if kt == 1:
                    ins.then_inc(S["pv_done"], 1)

            def up(r, o, s):
                es = experts_of(s)
                h = h_bank(r, o, s)
                if r[1] + o == PAIRS - 1 and s > 0:
                    pe.wait_ge(S["max_done"], 4 * HALVES)
                    pe.wait_ge(S["silu_ready"], at(r, lambda i: SLOTS * (i + o) + s - 1))
                    pe.wait_ge(S["branch_ready"], at(r, lambda i: SLOTS * (i + o) + s - 1))
                else:
                    pe.wait_ge(S["silu_ready"], at(r, lambda i: SLOTS * (i + o) + s))
                    pe.wait_ge(S["branch_ready"], at(r, lambda i: SLOTS * (i + o) + s))
                if s == 0:
                    pe.wait_ge(S["xt_ready"], at(r, lambda i: i + o + 1))
                    if r[1] + o == 0:
                        pe.wait_ge(S["w_ffn_in"], 16 * 5)
                for t, w in enumerate((w1, w3)):
                    for n, e in enumerate(es):
                        c0 = (2 * t + n) * P
                        for c in range(2):
                            ins = pe.matmul(h[:, c0:c0 + P], w[:, c, e * INTER:(e + 1) * INTER], xn2T[:, c, :],
                                            start=(c == 0), stop=(c == 1))
                ins.then_inc(S["up_done"], 1)

            def down(r, o, s):
                es = experts_of(s)
                if s == 0:
                    pe.wait_ge(S["hidden_ready"], at(r, lambda i: SLOTS * (i + o) + 1))
                    pe.wait_ge(S["res_ready"], at(r, lambda i: i + o))
                else:
                    pe.wait_ge(S["gated_ready"], at(r, lambda i: 4 * (i + o) + s))
                for n, e in enumerate(es):
                    ins = pe.matmul(y_ps[:, 0:T], gwt[:, s % 2, n, :], w2[:, e, :],
                                    start=(s == 0), stop=(s == SLOTS - 1 and n == 1))
                ins.then_inc(S["down_done"], 1)

            def qk(r):
                if r[1] == -1:
                    pe.wait_ge(S["w_qk_in"], 32)
                pe.wait_ge(S["xn_ready"], at(r, lambda i: i + 2))
                for t in range(2):
                    ins = pe.matmul(m_ps[:, T * t:T * t + T], wqk[:, t, :], xn[:, :], start=True, stop=True)
                ins.then_inc(S["qk_done"], 1)

            def project_v(r):
                pe.wait_ge(S["combt_ready"], at(r, lambda i: i - 1))
                pe.wait_ge(S["part1_ready"], at(r, lambda i: 2 * (i + 2)))
                pe.wait_ge(S["rest_ready"], at(r, lambda i: i + 2))
                if r[1] == -1:
                    pe.wait_ge(S["w_v_in"], 32)
                for kt in range(2):
                    ins = pe.matmul(m_ps[:, P * kt:P * kt + P], xn[:, P * kt:P * kt + P], wv[:, :], start=True, stop=True)
                ins.then_inc(S["v_done"], 1)

            def project_o(r):
                pe.wait_ge(S["vnext_ready"], at(r, lambda i: min(i + 2, PAIRS) if isinstance(i, int) else i + 2))
                if r[1] == 1:
                    pe.wait_ge(S["w_o_in"], 16)
                if r[1] == PAIRS:
                    pe.wait_ge(S["combt_ready"], PAIRS - 1)
                pe.wait_ge(S["oT_ready"], at(r, lambda i: 2 * i))
                for b in range(2):
                    for hh in range(2):
                        ins = pe.matmul(m_ps[C * b:C * b + C, 0:T], wo[:, hh, :], oT[:, b, T * hh:T * hh + T],
                                        start=(hh == 0), stop=(hh == 1))
                ins.then_inc(S["o_done"], 1)

            def project_ct(r):
                if r[1] == 1:
                    pe.wait_ge(S["w_ct_in"], 32)
                pe.wait_ge(S["y_ready"], at(r, lambda i: i))
                pe.matmul(m_ps[:, 0:T], wct[:, :], y[:, :], start=True, stop=True).then_inc(S["ct_done"], 1)

            def turn_x(r):
                pe.wait_ge(S["x2_ready"], at(r, lambda i: i))
                pe.wait_ge(S["xn2_ready"], at(r, lambda i: i))
                for c in range(2):
                    ins = pe.transpose(m_ps[:, P * c:P * c + P], xn2[:, P * c:P * c + P], ident[:, :])
                ins.then_inc(S["xt_done"], 1)

            def logits(r):
                if r[1] == 1:
                    pe.wait_ge(S["w_gate_in"], 16)
                pe.wait_ge(S["xt_ready"], at(r, lambda i: i))
                for c in range(2):
                    ins = pe.matmul(m_ps[0:NE, 0:P], gw[:, c, :], xn2T[:, c, :], start=(c == 0), stop=(c == 1))
                ins.then_inc(S["gt_done"], 1)

            def turn_logits(r):
                pe.wait_ge(S["gt_ready"], at(r, lambda i: i)).then_inc(S["held_tensor"], 1)
                pe.transpose(m_ps[:, 0:NE], gT[:, :], ident[0:NE, 0:NE]).then_inc(S["g_done"], 1)

            def turn_comb(r):
                pe.wait_ge(S["gdif_ready"], at(r, lambda i: i))
                if has_pair(r[1] + 2):
                    pe.wait_ge(S["part1_ready"], at(r, lambda i: 2 * (i + 3)))
                    pe.wait_ge(S["rest_ready"], at(r, lambda i: i + 3))
                pe.wait_ge(S["comb_ready"], at(r, lambda i: i))
                pe.transpose(m_ps[0:NE, 0:P], comb[:, :], ident[:, :]).then_inc(S["combt_done"], 1)

            def body(r):
                i, low = r
                mid, tail, new = has_pair(low - 1), has_pair(low - 2), has_pair(low + 1)
                last, final = low == PAIRS, low == PAIRS + 1
                for j in range(4):
                    here, ahead, rows, back = (has_half(4 * low + j + d) for d in (0, 2, 1, -1))

                    def s(n):
                        if ahead:
                            scores(r, j, n)

                    def t(n):
                        if n == 1 and rows:
                            turn_max(r, j)
                        if here:
                            scores_t(r, j, n)

                    def pv(*kts):
                        if back:
                            for kt in kts:
                                probs_v(r, j, kt)

                    s(0)
                    s(1)
                    t(0)
                    if j == 0:
                        if parts_step(j, r):
                            qk(r)
                        t(1)
                        pv(0, 1)
                        s(2)
                        s(3)
                        t(2)
                        if new:
                            project_v(r)
                        t(3)
                        if tail:
                            up(r, -2, 3)
                        if final:
                            up(r, -2, 4)
                    if j == 1:
                        if parts_step(j, r):
                            pe.wait_ge(S["vnext_ready"], 1)
                            qk(parts_step(j, r))
                        t(1)
                        if tail and not last:
                            down(r, -2, 1)
                        if mid:
                            project_o(r)
                        pv(0, 1)
                        s(2)
                        s(3)
                        t(2)
                        if mid:
                            project_ct(r)
                        if last:
                            down(r, -2, 1)
                        if tail and not final:
                            up(r, -2, 4)
                        t(3)
                        if tail:
                            down(r, -2, 2)
                    if j == 2:
                        t(1)
                        if mid:
                            turn_x(r)
                        if tail:
                            down(r, -2, 3)
                        s(2)
                        t(2)
                        s(3)
                        if mid:
                            logits(r)
                        t(3)
                        if mid:
                            up(r, -1, 0)
                        pv(0, 1)
                        if mid:
                            turn_logits(r)
                        if tail:
                            down(r, -2, 4)
                    if j == 3:
                        t(1)
                        if parts_step(j, r):
                            pe.wait_ge(S["vnext_ready"], at(r, lambda i: i + 2))
                            pe.wait_ge(S["gdif_ready"], at(r, lambda i: i))
                            qk(parts_step(j, r))
                        s(2)
                        if mid:
                            up(r, -1, 1)
                            down(r, -1, 0)
                        pv(0, 1)
                        s(3)
                        t(2)
                        t(3)
                        if last:
                            turn_comb(r)
                        if mid:
                            up(r, -1, 2)
                        if mid and not last:
                            turn_comb(r)

            run(pe, body)


DVE_LINKS = 16

_IN = ["x", "ctx_in", "w_qk", "b_qk", "w_v", "b_v", "w_o", "w_ct", "b_ct", "w_gate", "w_1", "w_3", "w_2"]


def kernel(x, ctx_2048, L0_xattn_w_in, L0_xattn_b_in, L0_xattn_w_out, L0_xattn_b_out, L0_xattn_w_ct, L0_xattn_b_ct,
           L0_ffn_gate_w, L0_ffn_w1, L0_ffn_w2, L0_ffn_w3, L0_ffn_ws1, L0_ffn_ws2, L0_ffn_ws3):
    import numpy as np
    import concourse.bacc as bacc
    from concourse.bass_utils import run_bass_kernel_spmd

    a = {k: np.asarray(t) for k, t in locals().items() if k not in ("np", "bacc", "run_bass_kernel_spmd")}
    w_in, b_in = a["L0_xattn_w_in"], a["L0_xattn_b_in"]

    def twice(m):
        z = np.zeros_like(m)
        return np.block([[m, z], [z, m]])

    q_k = w_in[:2 * C].reshape(2, H, D, C).transpose(0, 3, 2, 1).reshape(2, C, C)
    b_qk = b_in[:2 * C].reshape(2, H, D).transpose(2, 1, 0).reshape(C, 2)
    w_o = np.zeros((HG, 32, 2, C), w_in.dtype)
    w_o[:, :D] = a["L0_xattn_w_out"].T.reshape(2, HG, D, C).transpose(1, 2, 0, 3)
    w_o[0, D, 0] = a["L0_xattn_b_out"]
    ins = {
        "x": a["x"].reshape(B * C, T), "ctx_in": a["ctx_2048"].reshape(B * C, T),
        "w_qk": np.stack([twice(q_k[0]), twice(q_k[1])], axis=1), "b_qk": np.concatenate([b_qk, b_qk]),
        "w_v": twice(w_in[2 * C:].T), "b_v": np.tile(b_in[2 * C:], 4).reshape(1, 2 * P),
        "w_o": w_o.reshape(P, 2, C),
        "w_ct": twice(a["L0_xattn_w_ct"]), "b_ct": np.tile(a["L0_xattn_b_ct"], 2).reshape(P, 1),
        "w_gate": a["L0_ffn_gate_w"].T,
        "w_1": np.concatenate([a["L0_ffn_w1"].transpose(2, 0, 1).reshape(T, NE * INTER), a["L0_ffn_ws1"].T], axis=1),
        "w_3": np.concatenate([a["L0_ffn_w3"].transpose(2, 0, 1).reshape(T, NE * INTER), a["L0_ffn_ws3"].T], axis=1),
        "w_2": np.concatenate([a["L0_ffn_w2"].transpose(2, 0, 1), a["L0_ffn_ws2"].T[:, None]], axis=1),
    }
    nc = bacc.Bacc("TRN2", target_bir_lowering=False, num_devices=1)
    arrays, args = {}, []
    for name in _IN:
        t = np.ascontiguousarray(ins[name])
        arrays[f"in_{name}"] = t
        args.append(nc.dram_tensor(f"in_{name}", t.shape, mybir.dt.from_np(t.dtype), kind="ExternalInput").ap())
    args.append(nc.dram_tensor("out_0", (B * C, T), F32, kind="ExternalOutput").ap())
    build(nc, *args)
    r = run_bass_kernel_spmd(nc, [arrays], core_ids=[0])
    return r.results[0]["out_0"].reshape(B, C, T)
```
